# Optimizing a Trainium2 kernel written in Bass

```python
import numpy as np
import jax
import jax.numpy as jnp

def _softmax(x, axis=-1):
    return jax.nn.softmax(x, axis=axis)

def _gelu(x):
    return jax.nn.gelu(x, approximate=True)

def _silu(x):
    return jax.nn.silu(x)

def _sigmoid(x):
    return jax.nn.sigmoid(x)

def _layernorm(x, axis=-1, eps=1e-05):
    m = jnp.mean(x, axis=axis, keepdims=True)
    v = jnp.var(x, axis=axis, keepdims=True)
    return (x - m) / jnp.sqrt(v + eps)

def _scatter_add(tgt, idx, src, axis=0):
    return tgt.at[idx].add(src)

def _segment_sum(src, seg, n):
    return jax.ops.segment_sum(src, seg, n)
kernel_name = 'mk_recurrent_d1_jaxref_r2_116360'

def setup_inputs(seed: int=0):
    np.random.seed(seed)
    _w = jnp.asarray

    def _L0_attn_setup():
        import jax, jax.numpy as jnp
        import numpy as np

        def log_g(x):
            return jnp.where(x >= 0, jnp.log(jax.nn.relu(x) + 0.5), -jax.nn.softplus(-x))

        def _reference_tuple_inner(x, W1, b1, W2, b2, init_h):
            B, S, _ = x.shape
            Din = init_h.shape[0]
            proj = x @ W1 + b1
            hidden, forget_gate, input_gate = jnp.split(proj, 3, axis=-1)
            diff = jax.nn.softplus(-forget_gate) - jax.nn.softplus(-input_gate)
            log_coeffs = -jax.nn.softplus(diff)
            log_val_coeffs = -jax.nn.softplus(-diff)
            log_values = log_val_coeffs + log_g(hidden)
            prev_log_hidden = jnp.broadcast_to(log_g(init_h), (B, 1, Din))
            log_values = jnp.concatenate([prev_log_hidden, log_values], axis=1)
            log_coeffs = jnp.pad(log_coeffs, ((0, 0), (1, 0), (0, 0)))
            a_star = jnp.cumsum(log_coeffs, axis=1)
            log_h = a_star + jax.lax.cumlogsumexp(log_values - a_star, axis=1)
            out_h = jnp.exp(log_h[:, -S:])
            next_hidden = out_h[:, -1:]
            next_log_hidden = log_h[:, -1:]
            out = out_h @ W2 + b2
            return (out, next_hidden, next_log_hidden)
        key = jax.random.key(seed)
        ks = jax.random.split(key, 6)
        B, S, D, Din = (4, 2048, 512, 1024)
        x = jax.random.normal(ks[0], (B, S, D), jnp.float32)
        s1 = 1.0 / np.sqrt(D)
        W1 = jax.random.normal(ks[1], (D, 3 * Din), jnp.float32) * s1
        b1 = jax.random.normal(ks[2], (3 * Din,), jnp.float32) * s1
        b1 = b1.at[Din:2 * Din].add(1.0)
        s2 = 1.0 / np.sqrt(Din)
        W2 = jax.random.normal(ks[3], (Din, D), jnp.float32) * s2
        b2 = jax.random.normal(ks[4], (D,), jnp.float32) * s2
        init_h = jax.random.normal(ks[5], (Din,), jnp.float32)
        return {'x': x, 'W1': W1, 'b1': b1, 'W2': W2, 'b2': b2, 'init_h': init_h}
    _L0_attn_in = _L0_attn_setup()

    def _L0_ffn_setup():
        import jax, jax.numpy as jnp
        import numpy as np
        H = 512
        I = 1024
        E = 32
        B, S = (4, 1024)

        def _grouped_mm(a, w, group_sizes):
            return jax.lax.ragged_dot(a, w, group_sizes)

        def _swiglu(x, gw, uw, dw):
            return jax.nn.silu(x @ gw) * (x @ uw) @ dw
        key = jax.random.key(seed)
        ks = jax.random.split(key, 8)
        scale = 0.02
        inp = {'hidden_states': jax.random.normal(ks[0], (B, S, H), dtype=jnp.float32), 'gate_w': jax.random.normal(ks[1], (H, E), dtype=jnp.float32) * scale, 'shared_gate_w': jax.random.normal(ks[2], (H, I), dtype=jnp.float32) * scale, 'shared_up_w': jax.random.normal(ks[3], (H, I), dtype=jnp.float32) * scale, 'shared_down_w': jax.random.normal(ks[4], (I, H), dtype=jnp.float32) * scale, 'routed_gate_w': jax.random.normal(ks[5], (E, H, I), dtype=jnp.float32) * scale, 'routed_up_w': jax.random.normal(ks[6], (E, H, I), dtype=jnp.float32) * scale, 'routed_down_w': jax.random.normal(ks[7], (E, I, H), dtype=jnp.float32) * scale}
        return inp
    _L0_ffn_in = _L0_ffn_setup()
    _d = {'L0_attn_x': _L0_attn_in['x'], 'L0_attn_W1': _L0_attn_in['W1'], 'L0_attn_b1': _L0_attn_in['b1'], 'L0_attn_W2': _L0_attn_in['W2'], 'L0_attn_b2': _L0_attn_in['b2'], 'L0_attn_init_h': _L0_attn_in['init_h'], 'L0_ffn_gate_w': _L0_ffn_in['gate_w'], 'L0_ffn_shared_gate_w': _L0_ffn_in['shared_gate_w'], 'L0_ffn_shared_up_w': _L0_ffn_in['shared_up_w'], 'L0_ffn_shared_down_w': _L0_ffn_in['shared_down_w'], 'L0_ffn_routed_gate_w': _L0_ffn_in['routed_gate_w'], 'L0_ffn_routed_up_w': _L0_ffn_in['routed_up_w'], 'L0_ffn_routed_down_w': _L0_ffn_in['routed_down_w']}
    _x0 = _d['L0_attn_x']
    _d['L0_attn_x'] = jax.random.normal(jax.random.fold_in(jax.random.key(seed), 1), (8, 1024, 512), dtype=_x0.dtype)
    del _x0
    return _d

def reference(L0_attn_x, L0_attn_W1, L0_attn_b1, L0_attn_W2, L0_attn_b2, L0_attn_init_h, L0_ffn_gate_w, L0_ffn_shared_gate_w, L0_ffn_shared_up_w, L0_ffn_shared_down_w, L0_ffn_routed_gate_w, L0_ffn_routed_up_w, L0_ffn_routed_down_w):

    def _L0_attn_ref(x, W1, b1, W2, b2, init_h):
        import jax, jax.numpy as jnp
        import numpy as np

        def log_g(x):
            return jnp.where(x >= 0, jnp.log(jax.nn.relu(x) + 0.5), -jax.nn.softplus(-x))

        def _reference_tuple_inner(x, W1, b1, W2, b2, init_h):
            B, S, _ = x.shape
            Din = init_h.shape[0]
            proj = x @ W1 + b1
            hidden, forget_gate, input_gate = jnp.split(proj, 3, axis=-1)
            diff = jax.nn.softplus(-forget_gate) - jax.nn.softplus(-input_gate)
            log_coeffs = -jax.nn.softplus(diff)
            log_val_coeffs = -jax.nn.softplus(-diff)
            log_values = log_val_coeffs + log_g(hidden)
            prev_log_hidden = jnp.broadcast_to(log_g(init_h), (B, 1, Din))
            log_values = jnp.concatenate([prev_log_hidden, log_values], axis=1)
            log_coeffs = jnp.pad(log_coeffs, ((0, 0), (1, 0), (0, 0)))
            a_star = jnp.cumsum(log_coeffs, axis=1)
            log_h = a_star + jax.lax.cumlogsumexp(log_values - a_star, axis=1)
            out_h = jnp.exp(log_h[:, -S:])
            next_hidden = out_h[:, -1:]
            next_log_hidden = log_h[:, -1:]
            out = out_h @ W2 + b2
            return (out, next_hidden, next_log_hidden)
        return _reference_tuple_inner(x, W1, b1, W2, b2, init_h)[0]

    def _L0_ffn_ref(hidden_states, gate_w, shared_gate_w, shared_up_w, shared_down_w, routed_gate_w, routed_up_w, routed_down_w):
        import jax, jax.numpy as jnp
        import numpy as np
        H = 512
        I = 1024
        E = 32
        B, S = (4, 1024)

        def _grouped_mm(a, w, group_sizes):
            return jax.lax.ragged_dot(a, w, group_sizes)

        def _swiglu(x, gw, uw, dw):
            return jax.nn.silu(x @ gw) * (x @ uw) @ dw
        b, s, h = hidden_states.shape
        x = hidden_states.reshape(-1, h)
        shared_out = _swiglu(x, shared_gate_w, shared_up_w, shared_down_w)
        logits = x @ gate_w
        topk_ids = jnp.argmax(logits, axis=-1)
        topk_val = jnp.max(logits, axis=-1)
        scores = jax.nn.sigmoid(topk_val)[:, None]
        xs = x * scores
        tokens_per_expert = jnp.zeros((E,), jnp.int32).at[topk_ids].add(1)
        order = jnp.argsort(topk_ids)
        sorted_x = xs[order]
        g = _grouped_mm(sorted_x, routed_gate_w, tokens_per_expert)
        u = _grouped_mm(sorted_x, routed_up_w, tokens_per_expert)
        d = _grouped_mm(jax.nn.silu(g) * u, routed_down_w, tokens_per_expert)
        inv = jnp.argsort(order)
        routed_out = d[inv]
        return (shared_out + routed_out).reshape(b, s, h)
    x = L0_attn_x
    xn = _layernorm(x, axis=-1)
    s = _L0_attn_ref(xn, L0_attn_W1, L0_attn_b1, L0_attn_W2, L0_attn_b2, L0_attn_init_h)
    g = _silu(_L0_ffn_ref(xn, L0_ffn_gate_w, L0_ffn_shared_gate_w, L0_ffn_shared_up_w, L0_ffn_shared_down_w, L0_ffn_routed_gate_w, L0_ffn_routed_up_w, L0_ffn_routed_down_w))
    x = x + s * g
    return x

_drawn_inputs = setup_inputs


def setup_inputs(seed=0):
    import zlib

    import numpy as np

    out = dict(_drawn_inputs(seed))
    spreads = {}
    factors = {'L0_attn_W1': 4.117,
     'L0_attn_b1': 8.0,
     'L0_attn_b2': 8.0,
     'L0_attn_init_h': 8.0,
     'L0_ffn_gate_w': 3.762,
     'L0_ffn_routed_gate_w': 3.751,
     'L0_ffn_routed_up_w': 3.713,
     'L0_ffn_routed_down_w': 3.707,
     'L0_ffn_shared_gate_w': 3.348,
     'L0_ffn_shared_up_w': 3.277,
     'L0_ffn_shared_down_w': 3.277}
    for name, (base, spread) in spreads.items():
        noise = np.random.default_rng([zlib.crc32(name.encode()), seed]).standard_normal(out[name].shape)
        drawn = base * np.exp(spread * noise) if base else spread * noise
        out[name] = jnp.asarray(drawn.astype(out[name].dtype))
    for name, factor in factors.items():
        out[name] = (out[name] * factor).astype(out[name].dtype)
    return out
```

```python
from contextlib import ExitStack

import concourse.bass as bass
from concourse import mybir

ALU = mybir.AluOpType
ACT = mybir.ActivationFunctionType
F32 = mybir.dt.float32
F32R = mybir.dt.float32r
BF16 = mybir.dt.bfloat16
I32 = mybir.dt.int32
U32 = mybir.dt.uint32
AX_X = mybir.AxisListType.X
P = 128
CHUNK = 512
TILES = CHUNK // P
EPS = 1e-5


class Shapes:

    def __init__(self, x, W1, gate_w, sgw):
        self.B, self.S, self.D = x.shape
        self.T = self.B * self.S
        self.KD = self.D // P
        self.DIN = W1.shape[1] // 3
        self.NB = self.DIN // P
        self.E = gate_w.shape[1]
        self.I = sgw.shape[1]
        self.NI = self.I // P
        self.NCH = self.T // CHUNK
        self.NT = self.T // P
        self.NS = self.NT + self.E


class Kit:

    def __init__(self, nc, ctx):
        self.nc, self.ctx, self.sems = nc, ctx, []
        ctx.callback(self.clear)

    def clear(self):
        if self.sems:
            self.nc.clear_and_free_semaphores(self.sems)
            self.nc.all_engine_barrier()

    def sb(self, name, shape, dt=F32):
        return self.ctx.enter_context(self.nc.sbuf_tensor(name, shape, dt))

    def ps(self, name, shape, dt=F32):
        return self.ctx.enter_context(self.nc.psum_tensor(name, shape, dt))

    def sem(self, name):
        self.sems.append(self.nc.alloc_semaphore(name))
        return self.sems[-1]


def settle(eng, settled):
    eng.sem_inc(settled, 1)


def matmul_pairs(pe, out, w, x, start, stop):
    pe.matmul(out, w[0], x[0], start=start, stop=False)
    pe.matmul(out, w[0], x[1], start=False, stop=False)
    return pe.matmul(out, w[1], x[0], start=False, stop=stop)


def round_hi(act, hi, raw, done):
    act.activation(hi, raw, ACT.Copy).then_inc(done, 1)


def leave_lo(eng, lo, raw, hi, done):
    eng.tensor_tensor(lo, raw, hi, ALU.subtract).then_inc(done, 1)


def at_least(eng, sem, value):
    if not isinstance(value, int) or value > 0:
        eng.wait_ge(sem, value)


def shared_sweep(nc, z, x, gate_w, sgw, suw, sdw, xT_dram, xs_dram, ss_dram, onehot, ident):
    KD, NI, E, D, I, NCH = z.KD, z.NI, z.E, z.D, z.I, z.NCH
    x_v = x.rearrange("b s d -> (b s) d").rearrange("(c q p) d -> c p q d", q=TILES, p=P)
    xs_v = xs_dram.rearrange("(c q p) d -> c p q d", q=TILES, p=P)
    ss_t = ss_dram.rearrange("(t p) d -> t p d", p=P)
    with ExitStack() as ctx:
        k = Kit(nc, ctx)
        gup = [k.sb(f"gu_{h}", [P, 2, KD, I], F32R) for h in ("hi", "lo")]
        dnp = [k.sb(f"dn_{h}", [P, NI, D], F32R) for h in ("hi", "lo")]
        rt = k.sb("router", [P, KD, 2, E], F32R)
        QC = I // TILES
        y = k.sb("y_sb", [P, 2, D])
        assert 2 * D == KD * QC
        raw = [y[:].rearrange("p q d -> p (q d)"), k.sb("raw_weights", [P, KD * QC])[:]]
        order, parts = [], {}

        def part(key, hi_lo, src):
            stage = raw[len(order) % 2][:, 0:src.shape[1] * src.shape[2]]
            parts[key] = (hi_lo, src, stage.rearrange("p (a b) -> p a b", a=src.shape[1]))
            order.append(key)

        def down_part(n):
            ks = slice(n * NI // TILES, (n + 1) * NI // TILES)
            part(("down", n), [w[:, ks, :] for w in dnp], sdw.rearrange("(k p) d -> p k d", p=P)[:, ks, :])

        part("router", [rt[:, :, n, :] for n in range(2)], gate_w.rearrange("(k p) e -> p k e", p=P))
        for n in range(TILES):
            cols = slice(n * QC, (n + 1) * QC)
            for m, w in enumerate((sgw, suw)):
                part((m, n), [g[:, m, :, cols] for g in gup], w.rearrange("(k p) i -> p k i", p=P)[:, :, cols])
            if n > 0:
                down_part(n - 1)
        down_part(TILES - 1)

        x_in = k.sb("x_in", [P, 2, TILES, D])
        xn = k.sb("xn", [P, TILES, D])
        stats = k.sb("stats", [P, TILES, 6])
        mv = k.sb("mv", [P, 2, TILES, 2])
        std = k.sb("std", [P, TILES])
        r0 = k.sb("r0", [P, TILES])
        vr = k.sb("vr", [P, TILES])
        vrr = k.sb("vrr", [P, TILES])
        half = k.sb("half", [P, TILES])
        rstd = k.sb("rstd", [P, 2, TILES])
        rs = k.sb("rs", [P, TILES])
        xT = [k.sb(f"xT{j}", [P, 2, KD, CHUNK], F32R) for j in range(2)]
        logits = k.sb("logits", [P, TILES, E])
        top = k.sb("top", [P, TILES, 8])
        topi = k.sb("topi", [P, TILES, 8], U32)
        topf = k.sb("topf", [P, TILES])
        score = k.sb("score", [P, TILES])
        iota_e = k.sb("iota_e", [P, E])
        eps = k.sb("eps", [P, 1])
        h = k.sb("h_act", [P, 2, CHUNK])
        hT = k.sb("hT", [P, 2, NI, CHUNK], F32R)

        psG = [k.ps(f"psG{i}", [P, CHUNK]) for i in range(2)]
        psU = [k.ps(f"psU{i}", [P, CHUNK]) for i in range(2)]
        psY = [k.ps(f"psY{i}", [P, D]) for i in range(2)]
        psT = k.ps("psT", [P, KD, P])
        psL = k.ps("psL", [P, TILES, 2, E])

        x_loaded = [k.sem(f"x_loaded{j}") for j in range(2)]
        xs_stored = k.sem("xs_stored")
        xT_stored = [k.sem(f"xT_stored{j}") for j in range(2)]
        y_stored = [k.sem(f"y_stored{j}") for j in range(2)]
        stats_done = k.sem("stats_done")
        mv_done = k.sem("mv_done")
        std_done = k.sem("std_done")
        r0_done = k.sem("r0_done")
        newton = k.sem("newton")
        xn_done = k.sem("xn_done")
        xpose_done = k.sem("xpose_done")
        xhi_done = k.sem("xhi_done")
        xlo_done = k.sem("xlo_done")
        logits_mm = k.sem("logits_mm")
        logits_done = k.sem("logits_done")
        top_done = k.sem("top_done")
        topi_done = k.sem("topi_done")
        topf_done = k.sem("topf_done")
        onehot_done = k.sem("onehot_done")
        score_done = k.sem("score_done")
        xs_done = k.sem("xs_done")
        const_done = k.sem("const_done")
        settled = k.sem("settled1")
        rs_done = k.sem("rs_done")
        w_loaded = {key: k.sem(f"w_loaded{n}") for n, key in enumerate(order)}
        w_hi = k.sem("w_hi")
        w_lo = k.sem("w_lo")
        g_mm = k.sem("g_mm")
        u_mm = k.sem("u_mm")
        sg_done = k.sem("sg_done")
        h_done = k.sem("h_done")
        hhi_done = k.sem("hhi_done")
        hlo_done = k.sem("hlo_done")
        y_mm = k.sem("y_mm")
        y_copied = k.sem("y_copied")
        block = ctx.enter_context(nc.Block())

        def chunks(eng, one):
            for j in range(2):
                one(j, j, 0, True, NCH > 2)
            if NCH > 4:
                with eng.Fori(1, NCH // 2 - 1) as it:
                    for j in range(2):
                        one(it * 2 + j, j, it, True, True)
            it = NCH // 2 - 1
            for j in range(2):
                one(it * 2 + j, j, it, j == 0, False)

        def nxt(c, j, it):
            return c + 1, 1 - j, it + j

        def nxt2(c, j, it):
            return c + 2, j, it + 1

        def weights(c, b, split):
            if isinstance(c, int) and c == 0:
                if b % 2 == 0 and b + 2 < NI:
                    split((0, b // 2 + 1))
                    split((1, b // 2 + 1))
                elif b % 2 == 1:
                    split(("down", b // 2))

        @block.sync
        def _(sp):
            def load(c, j, it):
                at_least(sp, xs_stored, (c - 1) * 16)
                sp.dma_start(x_in[:, j], x_v[c]).then_inc(x_loaded[j], 16)

            def store_xT(c, j, it):
                sp.wait_ge(xlo_done, (c + 1) * TILES)
                sp.dma_start(xT_dram[c], xT[j][:].bitcast(F32)).then_inc(xT_stored[j], 16)

            def store_xs(c, j, it):
                sp.wait_ge(xs_done, (c + 1) * TILES)
                sp.dma_start(xs_v[c], x_in[:, j]).then_inc(xs_stored, 16)

            def one(c, j, it, more, more2):
                if more2 and not (isinstance(c, int) and c == 0):
                    load(*nxt2(c, j, it))
                if more:
                    store_xT(*nxt(c, j, it))
                for q in range(TILES):
                    if q == TILES // 2 and more:
                        store_xs(*nxt(c, j, it))
                    sp.wait_ge(y_copied, c * TILES + q + 1)
                    sp.dma_start(ss_t[c * TILES + q][:, 0:D], y[:, q % 2]).then_inc(y_stored[q % 2], 16)

            load(0, 0, 0)
            for n, key in enumerate(order):
                at_least(sp, w_lo, n - 1)
                sp.dma_start(parts[key][2], parts[key][1]).then_inc(w_loaded[key], 16)
                if n == 1:
                    load(1, 1, 0)
                elif key == ("down", 1):
                    store_xT(0, 0, 0)
                    store_xs(0, 0, 0)
                    if NCH > 2:
                        load(2, 0, 1)
            chunks(sp, one)
            sp.wait_ge(xs_stored, 16 * NCH)
            for j in range(2):
                sp.wait_ge(xT_stored[j], 16 * (NCH // 2))
                sp.wait_ge(y_stored[j], 16 * (NCH * TILES // 2))

        @block.gpsimd
        def _(pool):
            pool.iota(iota_e[:], [[1, E]], base=0, channel_multiplier=0,
                      allow_small_or_imprecise_dtypes=True).then_inc(const_done, 1)
            pool.memset(eps[:], EPS).then_inc(const_done, 1)
            pool.memset(ident[:], 0.0).then_inc(const_done, 1)
            pool.wait_ge(const_done, 3)
            pool.affine_select(out=ident[:], in_=ident[:], compare_op=ALU.not_equal, fill=1.0, base=0,
                               pattern=[[-1, P]], channel_multiplier=1).then_inc(const_done, 1)

            def prep(c, j, it):
                pool.wait_ge(r0_done, c + 1)
                settle(pool, settled)
                pool.tensor_scalar(vr[:], mv[:, j, :, 1], EPS, None, ALU.add).then_inc(newton, 1)
                pool.wait_ge(newton, c * 5 + 1)
                pool.tensor_tensor(vrr[:], vr[:], r0[:], ALU.mult).then_inc(newton, 1)
                pool.wait_ge(newton, c * 5 + 2)
                pool.tensor_tensor(half[:], vrr[:], r0[:], ALU.mult).then_inc(newton, 1)
                pool.wait_ge(newton, c * 5 + 3)
                settle(pool, settled)
                pool.tensor_scalar(vr[:], half[:], -0.5, 1.5, ALU.mult, ALU.add).then_inc(newton, 1)
                pool.wait_ge(newton, c * 5 + 4)
                at_least(pool, xn_done, (c - 1) * TILES)
                at_least(pool, rs_done, c - 1)
                pool.tensor_tensor(rstd[:, j], vr[:], r0[:], ALU.mult).then_inc(newton, 1)

            def scale(c, j, it):
                pool.wait_ge(score_done, c + 1)
                pool.wait_ge(newton, c * 5 + 5)
                at_least(pool, xs_done, c * TILES)
                pool.tensor_tensor(rs[:], rstd[:, j], score[:], ALU.mult).then_inc(rs_done, 1)
                pool.wait_ge(rs_done, c + 1)
                pool.wait_ge(xn_done, (c + 1) * TILES)
                settle(pool, settled)
                for q in range(TILES):
                    pool.tensor_scalar(x_in[:, j, q], x_in[:, j, q], mv[:, j, q, 0:1], rs[:, q:q + 1],
                                       ALU.subtract, ALU.mult).then_inc(xs_done, 1)

            def one(c, j, it, more, more2):
                if more2:
                    prep(*nxt2(c, j, it))
                if more:
                    scale(*nxt(c, j, it))

            prep(0, 0, 0)
            prep(1, 1, 0)
            scale(0, 0, 0)
            chunks(pool, one)

        @block.scalar
        def _(act):
            act.wait_ge(const_done, 4)

            def hi(key):
                act.wait_ge(w_loaded[key], 16)
                round_hi(act, parts[key][0][0], parts[key][2], w_hi)

            def roots(c, j, it):
                act.wait_ge(mv_done, (c + 1) * TILES)
                at_least(act, r0_done, c)
                act.activation(std[:], mv[:, j, :, 1], ACT.Sqrt, bias=eps[:, 0:1]).then_inc(std_done, 1)

            def x_hi(c, j, it, q):
                act.wait_ge(xpose_done, c * TILES + q + 1)
                if q == 0:
                    at_least(act, xT_stored[j], it * 16)
                    at_least(act, u_mm, (c - 1) * NI)
                act.activation(xT[j][:, 0, :, q * P:(q + 1) * P], psT[:], ACT.Copy).then_inc(xhi_done, 1)

            def scores(c, j, it):
                act.wait_ge(top_done, (c + 1) * TILES)
                at_least(act, rs_done, c)
                act.activation(score[:], top[:, :, 0], ACT.Sigmoid).then_inc(score_done, 1)

            def h_hi(c, b):
                act.wait_ge(h_done, c * NI + b + 1)
                if b == 0:
                    at_least(act, y_mm, c * TILES)
                act.activation(hT[:, 0, b], h[:, b % 2], ACT.Copy).then_inc(hhi_done, 1)

            def one(c, j, it, more, more2):
                for b in range(NI):
                    act.wait_ge(g_mm, c * NI + b + 1)
                    at_least(act, hhi_done, c * NI + b - 1)
                    at_least(act, hlo_done, c * NI + b - 1)
                    act.activation(h[:, b % 2], psG[b % 2][:], ACT.Silu).then_inc(sg_done, 1)
                    if b >= 1:
                        h_hi(c, b - 1)
                    if more and b % 2 == 0:
                        x_hi(*nxt(c, j, it), b // 2)
                    weights(c, b, hi)
                h_hi(c, NI - 1)
                if more2:
                    roots(*nxt2(c, j, it))
                if more:
                    scores(*nxt(c, j, it))
                for q in range(TILES):
                    act.wait_ge(y_mm, c * TILES + q + 1)
                    at_least(act, y_stored[q % 2], (c * (TILES // 2) + q // 2) * 16)
                    act.activation(y[:, q % 2], psY[q % 2][:], ACT.Copy).then_inc(y_copied, 1)

            roots(0, 0, 0)
            hi("router")
            for q in range(TILES):
                x_hi(0, 0, 0, q)
            hi((0, 0))
            hi((1, 0))
            roots(1, 1, 0)
            scores(0, 0, 0)
            chunks(act, one)

        @block.vector
        def _(dve):
            dve.wait_ge(const_done, 4)

            def lo(key):
                dve.wait_ge(w_hi, order.index(key) + 1)
                (hi_part, lo_part), _, raw_part = parts[key]
                leave_lo(dve, lo_part, raw_part, hi_part, w_lo)

            def stats_of(c, j, it, q):
                if q == 0:
                    dve.wait_ge(x_loaded[j], (it + 1) * 16)
                    at_least(dve, mv_done, c * TILES)
                dve.bn_stats(stats[:, q], x_in[:, j, q]).then_inc(stats_done, 1)

            def moments(c, j, it):
                dve.wait_ge(stats_done, (c + 1) * TILES)
                at_least(dve, xs_done, (c - 1) * TILES)
                at_least(dve, xn_done, (c - 1) * TILES)
                settle(dve, settled)
                for q in range(TILES):
                    dve.bn_aggr(mv[:, j, q], stats[:, q]).then_inc(mv_done, 1)

            def normalise(c, j, it):
                dve.wait_ge(std_done, c + 1)
                at_least(dve, newton, c * 5)
                dve.reciprocal(r0[:], std[:]).then_inc(r0_done, 1)
                dve.wait_ge(newton, c * 5 + 5)
                at_least(dve, xpose_done, c * TILES)
                for q in range(TILES):
                    dve.tensor_scalar(xn[:, q], x_in[:, j, q], mv[:, j, q, 0:1], rstd[:, j, q:q + 1],
                                      ALU.subtract, ALU.mult).then_inc(xn_done, 1)

            def x_lo(c, j, it, q):
                dve.wait_ge(xhi_done, c * TILES + q + 1)
                sl = slice(q * P, (q + 1) * P)
                dve.tensor_tensor(xT[j][:, 1, :, sl], psT[:], xT[j][:, 0, :, sl], ALU.subtract)\
                    .then_inc(xlo_done, 1)

            def route(c, j, it):
                dve.wait_ge(logits_mm, (c + 1) * TILES)
                at_least(dve, topi_done, c * TILES)
                dve.tensor_reduce(logits[:], psL[:].rearrange("p q h e -> p q e h"), AX_X, ALU.add)\
                    .then_inc(logits_done, 1)
                dve.wait_ge(logits_done, c + 1)
                at_least(dve, score_done, c)
                settle(dve, settled)
                for q in range(TILES):
                    dve.max(top[:, q], logits[:, q]).then_inc(top_done, 1)
                dve.wait_ge(top_done, (c + 1) * TILES)
                at_least(dve, topf_done, c)
                settle(dve, settled)
                for q in range(TILES):
                    dve.max_index(topi[:, q], top[:, q], logits[:, q]).then_inc(topi_done, 1)
                dve.wait_ge(topi_done, (c + 1) * TILES)
                at_least(dve, onehot_done, c * TILES)
                dve.tensor_copy(topf[:], topi[:, :, 0]).then_inc(topf_done, 1)
                dve.wait_ge(topf_done, c + 1)
                for q in range(TILES):
                    dve.tensor_scalar(onehot[:, bass.ds(c * TILES + q, 1), :].rearrange("p a e -> p (a e)"),
                                      iota_e[:], topf[:, q:q + 1], None, ALU.is_equal).then_inc(onehot_done, 1)

            def h_mul(c, b):
                dve.wait_ge(sg_done, c * NI + b + 1)
                dve.wait_ge(u_mm, c * NI + b + 1)
                dve.tensor_tensor(h[:, b % 2], h[:, b % 2], psU[b % 2][:], ALU.mult).then_inc(h_done, 1)

            def h_lo(c, b):
                dve.wait_ge(hhi_done, c * NI + b + 1)
                dve.tensor_tensor(hT[:, 1, b], h[:, b % 2], hT[:, 0, b], ALU.subtract).then_inc(hlo_done, 1)

            def one(c, j, it, more, more2):
                for b in range(NI):
                    h_mul(c, b)
                    if b >= 1:
                        h_lo(c, b - 1)
                    if more and b % 2 == 0:
                        x_lo(*nxt(c, j, it), b // 2)
                    weights(c, b, lo)
                    if more2 and b >= NI - TILES:
                        stats_of(*nxt2(c, j, it), b - NI + TILES)
                h_lo(c, NI - 1)
                if more2:
                    moments(*nxt2(c, j, it))
                if more:
                    route(*nxt(c, j, it))
                if more2:
                    normalise(*nxt2(c, j, it))

            def start(c):
                for q in range(TILES):
                    stats_of(c, c, 0, q)
                moments(c, c, 0)

            start(0)
            normalise(0, 0, 0)
            lo("router")
            for q in range(TILES):
                x_lo(0, 0, 0, q)
            lo((0, 0))
            lo((1, 0))
            start(1)
            route(0, 0, 0)
            normalise(1, 1, 0)
            chunks(dve, one)

        @block.tensor
        def _(pe):
            pe.wait_ge(const_done, 4)

            def transposes(c, j, it, q):
                pe.wait_ge(xn_done, c * TILES + q + 1)
                at_least(pe, xlo_done, c * TILES + q)
                for kb in range(KD):
                    mm = pe.transpose(psT[:, kb, :], xn[:, q, kb * P:(kb + 1) * P], ident[:])
                mm.then_inc(xpose_done, 1)

            def router(c, j, it, q):
                pe.wait_ge(xlo_done, c * TILES + q + 1)
                if q == 0:
                    at_least(pe, logits_done, c)
                sl = slice(q * P, (q + 1) * P)
                for kb in range(KD):
                    for a in range(2):
                        mm = pe.matmul(psL[:, q].rearrange("p h e -> p (h e)"), xT[j][:, a, kb, sl],
                                       rt[:, kb].rearrange("p h e -> p (h e)"),
                                       start=(kb == 0 and a == 0), stop=(kb == KD - 1 and a == 1))
                mm.then_inc(logits_mm, 1)

            def one(c, j, it, more, more2):
                first = isinstance(c, int) and c == 0
                for b in range(NI):
                    cols = slice(b * P, (b + 1) * P)
                    for m, bank, done, freed in ((0, psG[b % 2], g_mm, sg_done), (1, psU[b % 2], u_mm, h_done)):
                        if first and b % 2 == 0:
                            pe.wait_ge(w_lo, order.index((m, b // 2)) + 1)
                        at_least(pe, freed, c * NI + b - 1)
                        for kb in range(KD):
                            mm = matmul_pairs(pe, bank[:], (gup[0][:, m, kb, cols], gup[1][:, m, kb, cols]),
                                              (xT[j][:, 0, kb, :], xT[j][:, 1, kb, :]), kb == 0, kb == KD - 1)
                        mm.then_inc(done, 1)
                    if more and b % 2 == 0:
                        transposes(*nxt(c, j, it), b // 2)
                    if more and b % 2 == 1:
                        router(*nxt(c, j, it), b // 2)
                for q in range(TILES):
                    sl = slice(q * P, (q + 1) * P)
                    at_least(pe, y_copied, c * TILES + q - 1)
                    for kb in range(NI):
                        if q == 0:
                            pe.wait_ge(hlo_done, c * NI + kb + 1)
                            if first and kb % 2 == 0:
                                pe.wait_ge(w_lo, order.index(("down", kb // 2)) + 1)
                        mm = matmul_pairs(pe, psY[q % 2][:], (hT[:, 0, kb, sl], hT[:, 1, kb, sl]),
                                          (dnp[0][:, kb, :], dnp[1][:, kb, :]), kb == 0, kb == NI - 1)
                    mm.then_inc(y_mm, 1)

            pe.wait_ge(w_lo, 1)
            for q in range(TILES):
                transposes(0, 0, 0, q)
                router(0, 0, 0, q)
            chunks(pe, one)


def routing(nc, z, onehot, tok_dram, slot, token, tile_expert, tile_switch):
    NT, E, NS, T = z.NT, z.E, z.NS, z.T
    N = NT * E
    with ExitStack() as ctx:
        k = Kit(nc, ctx)
        before = k.sb("before", [P, P], BF16)
        ones_b = k.sb("ones_b", [P, P], BF16)
        ones = k.sb("ones", [P, N])
        tot = k.sb("tot", [P, E, NT])
        incl = k.sb("incl", [P, E, NT])
        excl = k.sb("excl", [P, E, NT])
        base = k.sb("base", [P, E, NT])
        cand = k.sb("cand", [P, NT, E])
        count = k.sb("count", [P, E])
        count_i = k.sb("count_i", [P, E], I32)
        tiles_i = k.sb("tiles_i", [P, E], I32)
        tiles_f = k.sb("tiles_f", [P, E])
        first_i = k.sb("first_incl", [P, E])
        first = k.sb("first", [P, E + 1])
        off = k.sb("off", [P, E])
        slot_f = k.sb("slot_f", [P, NT])
        iota_s = k.sb("iota_s", [1, NS + 1])
        tile_f = k.sb("tile_f", [1, 2, NS + 1])
        diff = k.sb("diff", [1, NS])
        diff2 = k.sb("diff2", [1, NS])
        fill = k.sb("fill", [NS, P], I32)
        psW = k.ps("psW", [P, N])
        psC = k.ps("psC", [P, N])
        const = k.sem("rconst")
        chain = k.sem("rchain")
        ranks = k.sem("ranks")
        filled = k.sem("filled")
        block = ctx.enter_context(nc.Block())

        @block.gpsimd
        def _(pool):
            pool.memset(before[:], 1.0).then_inc(const, 1)
            pool.memset(ones_b[:], 1.0).then_inc(const, 1)
            pool.memset(ones[:], 1.0).then_inc(const, 1)
            pool.memset(fill[:], T).then_inc(const, 1)
            pool.iota(token[:], [[P, NT]], base=0, channel_multiplier=1).then_inc(const, 1)
            pool.iota(iota_s[:], [[1, NS + 1]], base=0, channel_multiplier=0,
                      allow_small_or_imprecise_dtypes=True).then_inc(const, 1)
            pool.wait_ge(const, 6)
            pool.affine_select(out=before[:], in_=before[:], compare_op=ALU.is_gt, fill=0.0, base=0,
                               pattern=[[1, P]], channel_multiplier=-1).then_inc(const, 1)

        @block.sync
        def _(sp):
            sp.wait_ge(const, 4)
            sp.dma_start(tok_dram.rearrange("(s p) a -> s (p a)", p=P), fill[:]).then_inc(filled, 16)
            sp.wait_ge(filled, 16)

        @block.tensor
        def _(pe):
            pe.wait_ge(const, 7)
            cols = onehot[:].rearrange("p t e -> p (t e)")
            for a in range(0, N, 512):
                b = min(a + 512, N)
                pe.matmul(psC[:, a:b], ones_b[:], cols[:, a:b], start=True, stop=True)
            for a in range(0, N, 512):
                b = min(a + 512, N)
                mm = pe.matmul(psW[:, a:b], before[:], cols[:, a:b], start=True, stop=True)
            mm.then_inc(ranks, 1)

        @block.vector
        def _(dve):
            step = [0]

            def link(ins):
                step[0] += 1
                ins.then_inc(chain, 1)
                dve.wait_ge(chain, step[0])

            dve.wait_ge(const, 7)
            dve.wait_ge(ranks, 1)
            link(dve.tensor_copy(tot[:], psC[:].rearrange("p (t e) -> p e t", e=E)))
            flat = lambda a: a[:].rearrange("p e t -> p (e t)")
            link(dve.tensor_tensor_scan(flat(incl), ones[:], flat(tot), 0.0, ALU.mult, ALU.add))
            link(dve.tensor_tensor(flat(excl), flat(incl), flat(tot), ALU.subtract))
            link(dve.tensor_tensor(count[:], incl[:, :, NT - 1], excl[:, :, 0], ALU.subtract))
            link(dve.tensor_scalar(count[:], count[:], float(P - 1), None, ALU.add))
            link(dve.tensor_copy(count_i[:], count[:]))
            link(dve.tensor_single_scalar(tiles_i[:], count_i[:], P.bit_length() - 1, ALU.arith_shift_right))
            link(dve.tensor_copy(tiles_f[:], tiles_i[:]))
            link(dve.tensor_scalar(tiles_f[:], tiles_f[:], 1.0, None, ALU.max))
            link(dve.tensor_tensor_scan(first_i[:], ones[:, 0:E], tiles_f[:], 0.0, ALU.mult, ALU.add))
            link(dve.tensor_tensor(first[:, 0:E], first_i[:], tiles_f[:], ALU.subtract))
            link(dve.tensor_copy(first[:, E:E + 1], first_i[:, E - 1:E]))
            link(dve.scalar_tensor_tensor(off[:], first[:, 0:E], float(P), excl[:, :, 0], ALU.mult, ALU.subtract))
            for e in range(E):
                ins = dve.tensor_scalar(base[:, e, :], excl[:, e, :], off[:, e:e + 1], None, ALU.add)
            link(ins)
            link(dve.tensor_tensor(cand[:], psW[:].rearrange("p (t e) -> p t e", e=E),
                                   base[:].rearrange("p e t -> p t e"), ALU.add))
            link(dve.tensor_tensor(cand[:], cand[:], onehot[:], ALU.mult))
            link(dve.tensor_reduce(slot_f[:], cand[:], AX_X, ALU.add))
            link(dve.tensor_copy(slot[:], slot_f[:]))
            link(dve.memset(tile_f[:, 0, :], -1.0))
            for e in range(E + 1):
                link(dve.scalar_tensor_tensor(tile_f[:, (e + 1) % 2, :], iota_s[:], first[0:1, e:e + 1],
                                              tile_f[:, e % 2, :], ALU.is_ge, ALU.add))
            last = tile_f[:, (E + 1) % 2, :]
            link(dve.tensor_copy(tile_expert[:, 0:NS + 1], last))
            link(dve.tensor_copy(tile_expert[:, NS + 1:NS + 2], first[0:1, E:E + 1]))
            link(dve.tensor_tensor(diff[:], last[:, 1:NS + 1], last[:, 0:NS], ALU.subtract))
            link(dve.scalar_tensor_tensor(diff2[:], last[:, 1:NS + 1], float(E), diff[:], ALU.is_lt, ALU.mult))
            link(dve.tensor_copy(tile_switch[:], diff2[:]))


def recurrence_sweep(nc, z, xT_dram, W1, b1, W2, b2, init_h, ss_dram, slot, token, tok_dram):
    KD, NB, D, B, NCH = z.KD, z.NB, z.D, z.B, z.NCH
    CPS = z.S // CHUNK
    UPS = CPS * NB
    ss_t = ss_dram.rearrange("(t p) d -> t p d", p=P)
    GI, GF, GH = 2, 1, 0
    with ExitStack() as ctx:
        k = Kit(nc, ctx)
        w1 = [k.sb(f"w1_{h}", [P, KD, 3 * z.DIN], F32R) for h in ("hi", "lo")]
        w2 = [k.sb(f"w2_{h}", [P, NB, D], F32R) for h in ("hi", "lo")]
        w1v = W1.rearrange("(k p) n -> p k n", p=P)
        w2v = W2.rearrange("(k p) n -> p k n", p=P)

        def w1_part(w, kb):
            return w.rearrange("p k (g n) -> p k g n", g=3)[:, :, :, kb * P:(kb + 1) * P]

        b1s = k.sb("b1s", [P, 3 * NB])
        nbf = k.sb("nbf", [P, NB])
        bh5 = k.sb("bh5", [P, NB])
        b2row = k.sb("b2row", [1, D])
        b2all = k.sb("b2all", [P, D])
        one_row = k.sb("one_row", [1, P])
        one = k.sb("one", [P, 1])
        start = k.sb("start", [P, NB])
        state = k.sb("state", [P, NB])
        i0, i1, i2 = (k.sb(f"init{n}", [P, NB]) for n in range(3))
        isb = k.sb("isb", [P, CHUNK])
        m1 = k.sb("m1", [P, CHUNK])
        eu = k.sb("eu", [P, CHUNK])
        ev = k.sb("ev", [P, CHUNK])
        en = k.sb("en", [P, CHUNK])
        pa = k.sb("pa", [P, CHUNK])
        qb = k.sb("qb", [P, CHUNK])
        dn = k.sb("dn", [P, CHUNK])
        hm = k.sb("hm", [P, CHUNK])
        hp = k.sb("hp", [P, CHUNK])
        el = k.sb("el", [P, CHUNK])
        sd = k.sb("sd", [P, CHUNK])
        gg = k.sb("gg", [P, CHUNK])
        hs = k.sb("hs", [P, CHUNK])
        hT = k.sb("rhT", [P, 2, CHUNK], F32R)
        xT = [k.sb(f"rxT{j}", [P, 2, KD, CHUNK], F32R) for j in range(2)]
        y = k.sb("ry", [P, TILES, D])
        assert KD * 3 * P <= 3 * D and TILES == 4
        raw1 = y[:, 0:3].rearrange("p q d -> p (q d)")[:, 0:KD * 3 * P].rearrange("p (k g n) -> p k g n", k=KD, g=3)
        raw2 = y[:, 3]
        gate = [k.ps(f"gate{n}", [P, CHUNK]) for n in range(4)]
        psY = [k.ps(f"rpsY{q}", [P, D]) for q in range(TILES)]

        small = k.sem("small")
        prep = k.sem("prep")
        names = ("i_mm f_mm h_mm out_mm isb_done m1_done du_done dv_done eu_done ev_done en_done q_done "
                 "p_done d_done ln_done r_done hm_done hp_done eh_done l_done sd_done sig_done g_done "
                 "a_done c_done b_done scan_done state_done hi_done lo_done y_mm y_done")
        s = {n: k.sem(f"rec_{n}") for n in names.split()}
        (i_mm, f_mm, h_mm, out_mm, isb_done, m1_done, du_done, dv_done, eu_done, ev_done, en_done, q_done,
         p_done, d_done, ln_done, r_done, hm_done, hp_done, eh_done, l_done, sd_done, sig_done, g_done,
         a_done, c_done, b_done, scan_done, state_done, hi_done, lo_done, y_mm, y_done) = \
            (s[n] for n in names.split())
        xT_loaded = [k.sem(f"rec_xT_loaded{j}") for j in range(2)]
        y_stored = [k.sem(f"rec_y_stored{q}") for q in range(TILES)]
        b2_mm = k.sem("b2_mm")
        table_written = k.sem("table_written")
        settled = k.sem("settled2")
        w1_loaded, w2_loaded = k.sem("w1_loaded"), k.sem("w2_loaded")
        w1_hi, w1_lo, w2_hi, w2_lo = (k.sem(n) for n in ("w1_hi", "w1_lo", "w2_hi", "w2_lo"))

        def bias(g, kb):
            return b1s[:, g * NB + kb:g * NB + kb + 1]

        def sequences(eng, body):
            body(0, 0, True)
            with eng.Fori(1, B) as seq:
                body(seq * UPS, seq, False)

        block = ctx.enter_context(nc.Block())

        @block.sync
        def _(sp):
            sp.dma_start(b1s[:], b1.rearrange("(g p) -> p g", p=P),
                         allow_slow_non_contiguous=True).then_inc(small, 16)
            sp.dma_start(b2row[:], b2.rearrange("(a n) -> a n", a=1)).then_inc(small, 16)
            sp.dma_start(i0[:], init_h.rearrange("(g p) -> p g", p=P),
                         allow_slow_non_contiguous=True).then_inc(small, 16)

            def load(c, j, n, first):
                if not first:
                    sp.wait_ge(h_mm, (c - 1) * NB)
                sp.dma_start(xT[j][:].bitcast(F32), xT_dram[c]).then_inc(xT_loaded[j], 16)

            def store(c):
                for q in range(TILES):
                    tile = c * TILES + q
                    sp.wait_ge(y_done, tile + 1)
                    sp.dma_start(ss_t[tile][:, D:2 * D], y[:, q]).then_inc(y_stored[q], 16)

            def body(u0, seq, first):
                c0 = seq * CPS
                for j in range(CPS):
                    if not (first and j == 0):
                        store(c0 + j - 1)
                    if first and j == 0:
                        load(1, 1, 0, True)
                    elif first:
                        load(2, 0, 1, False)
                    else:
                        load(c0 + j + 1, 1 - j, seq + j, False)

            def load_weights(kb):
                at_least(sp, w2_lo, kb)
                for kk in range(KD):
                    sp.dma_start(raw1[:, kk], w1_part(w1v, kb)[:, kk]).then_inc(w1_loaded, 16)
                sp.dma_start(raw2, w2v[:, kb, :]).then_inc(w2_loaded, 16)

            load_weights(0)
            load(0, 0, 0, True)
            for kb in range(1, NB):
                load_weights(kb)
            body(0, 0, True)
            if B > 2:
                with sp.Fori(1, B - 1) as seq:
                    body(seq * UPS, seq, False)
            c0 = (B - 1) * CPS
            store(c0 - 1)
            load(c0 + 1, 1, B - 1, False)
            store(c0)
            store(c0 + 1)
            sp.wait_ge(table_written, 16 * z.NT)
            for q in range(TILES):
                sp.wait_ge(y_stored[q], 16 * NCH)

        @block.gpsimd
        def _(pool):
            pool.memset(one_row[:], 1.0).then_inc(prep, 1)
            pool.memset(one[:], 1.0).then_inc(prep, 1)

            def tail(U, kb):
                pool.wait_ge(g_done, U + 1)
                pool.wait_ge(c_done, U + 1)
                pool.tensor_tensor(qb[:], qb[:], gg[:], ALU.mult).then_inc(b_done, 1)
                pool.wait_ge(scan_done, U + 1)
                settle(pool, settled)
                pool.tensor_copy(state[:, kb:kb + 1], hs[:, CHUNK - 1:CHUNK]).then_inc(state_done, 1)

            def body(u0, seq, first):
                for n in range(UPS):
                    U, kb = u0 + n, n % NB
                    if not (first and n == 0):
                        tail(U - 1, (n - 1) % NB)
                    if first:
                        for t in range(n * z.NT // UPS, (n + 1) * z.NT // UPS):
                            pool.indirect_dma_start(
                                out=tok_dram, out_offset=bass.IndirectOffsetOnAxis(ap=slot[:, t:t + 1], axis=0),
                                in_=token[:, t:t + 1], in_offset=None).then_inc(table_written, 16)
                    pool.wait_ge(p_done, U + 1)
                    pool.wait_ge(q_done, U + 1)
                    pool.wait_ge(a_done, U)
                    pool.wait_ge(c_done, U)
                    pool.tensor_tensor(dn[:], pa[:], qb[:], ALU.add).then_inc(d_done, 1)
                    pool.wait_ge(l_done, U + 1)
                    pool.wait_ge(hm_done, U + 1)
                    pool.wait_ge(g_done, U)
                    pool.tensor_tensor(sd[:], hm[:], el[:], ALU.subtract).then_inc(sd_done, 1)
                    pool.wait_ge(r_done, U + 1)
                    pool.tensor_tensor(qb[:], qb[:], dn[:], ALU.mult).then_inc(c_done, 1)

            sequences(pool, body)
            tail(B * UPS - 1, NB - 1)

        @block.scalar
        def _(act):
            act.wait_ge(small, 48)
            act.wait_ge(prep, 3)
            act.activation(i2[:], i1[:], ACT.Exp).then_inc(prep, 1)
            act.wait_ge(prep, 4)
            act.activation(i2[:], i2[:], ACT.Ln, bias=one[:, 0:1]).then_inc(prep, 1)
            act.wait_ge(prep, 6)
            act.activation(i2[:], i2[:], ACT.Exp).then_inc(prep, 1)
            act.wait_ge(prep, 11)

            def split(U):
                act.wait_ge(scan_done, U + 1)
                act.wait_ge(out_mm, U)
                act.activation(hT[:, 0, :], hs[:], ACT.Copy).then_inc(hi_done, 1)

            def hi(kb):
                act.wait_ge(w1_loaded, (kb + 1) * 16 * KD)
                round_hi(act, w1_part(w1[0][:], kb), raw1, w1_hi)
                act.wait_ge(w2_loaded, (kb + 1) * 16)
                round_hi(act, w2[0][:, kb, :], raw2, w2_hi)

            hi(0)
            hi(1)

            def body(u0, seq, first):
                act.preload_act_table_set("natural_log_exp_and_others")
                for n in range(UPS):
                    U, kb = u0 + n, n % NB
                    act.wait_ge(i_mm, U + 1)
                    act.wait_ge(dv_done, U)
                    act.activation(isb[:], gate[(3 * n) % 4][:], ACT.Identity, bias=bias(GI, kb))\
                        .then_inc(isb_done, 1)
                    if not (first and n == 0):
                        split(U - 1)
                    act.wait_ge(m1_done, U + 1)
                    act.wait_ge(p_done, U)
                    act.wait_ge(q_done, U)
                    act.activation(en[:], m1[:], ACT.Exp).then_inc(en_done, 1)
                    act.wait_ge(du_done, U + 1)
                    act.activation(eu[:], eu[:], ACT.Exp, bias=nbf[:, kb:kb + 1]).then_inc(eu_done, 1)
                    act.wait_ge(dv_done, U + 1)
                    act.activation(ev[:], ev[:], ACT.Exp).then_inc(ev_done, 1)
                    act.wait_ge(h_mm, U + 1)
                    act.wait_ge(g_done, U)
                    act.activation(hp[:], gate[(3 * n + 2) % 4][:], ACT.Identity, bias=bh5[:, kb:kb + 1])\
                        .then_inc(hp_done, 1)
                    act.wait_ge(hm_done, U + 1)
                    act.wait_ge(sd_done, U)
                    act.activation(el[:], hm[:], ACT.Exp).then_inc(eh_done, 1)
                    act.wait_ge(eh_done, U + 1)
                    act.activation(el[:], el[:], ACT.Ln, bias=one[:, 0:1]).then_inc(l_done, 1)
                    act.wait_ge(d_done, U + 1)
                    act.activation(dn[:], dn[:], ACT.Ln).then_inc(ln_done, 1)
                    act.wait_ge(ln_done, U + 1)
                    act.activation(dn[:], dn[:], ACT.Exp, scale=-1.0).then_inc(r_done, 1)
                    act.wait_ge(sd_done, U + 1)
                    act.activation(sd[:], sd[:], ACT.Exp).then_inc(sig_done, 1)
                    if first and n + 2 < NB:
                        hi(n + 2)

            sequences(act, body)
            split(B * UPS - 1)

        @block.vector
        def _(dve):
            dve.wait_ge(small, 48)
            dve.wait_ge(prep, 2)
            dve.tensor_scalar(i1[:], i0[:], 0.0, None, ALU.min).then_inc(prep, 1)
            dve.wait_ge(prep, 5)
            dve.tensor_tensor(i2[:], i1[:], i2[:], ALU.subtract).then_inc(prep, 1)
            dve.wait_ge(prep, 7)
            dve.scalar_tensor_tensor(start[:], i0[:], 0.5, i2[:], ALU.add, ALU.max).then_inc(prep, 1)
            dve.tensor_scalar(nbf[:], b1s[:, GF * NB:(GF + 1) * NB], -1.0, None, ALU.mult).then_inc(prep, 1)
            dve.tensor_scalar(bh5[:], b1s[:, GH * NB:(GH + 1) * NB], 0.5, None, ALU.add).then_inc(prep, 1)
            dve.wait_ge(b2_mm, 1)
            dve.tensor_copy(b2all[:], psY[0][:]).then_inc(prep, 1)
            dve.wait_ge(prep, 11)

            def scan(U, n):
                kb = n % NB
                dve.wait_ge(b_done, U + 1)
                dve.wait_ge(a_done, U + 1)
                dve.wait_ge(state_done, U)
                dve.wait_ge(hi_done, U)
                dve.wait_ge(lo_done, U)
                first = start if n < NB else state
                dve.tensor_tensor_scan(hs[:], pa[:], qb[:], first[:, kb:kb + 1], ALU.mult, ALU.add)\
                    .then_inc(scan_done, 1)

            def split(U):
                dve.wait_ge(hi_done, U + 1)
                dve.tensor_tensor(hT[:, 1, :], hs[:], hT[:, 0, :], ALU.subtract).then_inc(lo_done, 1)

            def output(c):
                for q in range(TILES):
                    if q < TILES - 1:
                        dve.wait_ge(y_mm, c * (TILES - 1) + q + 1)
                    else:
                        dve.wait_ge(out_mm, (c + 1) * NB)
                    dve.wait_ge(y_stored[q], c * 16)
                    dve.tensor_tensor(y[:, q], psY[q][:], b2all[:], ALU.add).then_inc(y_done, 1)

            def lo(kb):
                dve.wait_ge(w1_hi, kb + 1)
                leave_lo(dve, w1_part(w1[1][:], kb), raw1, w1_part(w1[0][:], kb), w1_lo)
                dve.wait_ge(w2_hi, kb + 1)
                leave_lo(dve, w2[1][:, kb, :], raw2, w2[0][:, kb, :], w2_lo)

            lo(0)
            lo(1)

            def body(u0, seq, first):
                for n in range(UPS):
                    U, kb = u0 + n, n % NB
                    lag = not (first and n == 0)
                    if lag:
                        scan(U - 1, (n - 1) % UPS)
                    dve.wait_ge(f_mm, U + 1)
                    dve.wait_ge(isb_done, U + 1)
                    dve.wait_ge(en_done, U)
                    dve.wait_ge(du_done, U)
                    dve.wait_ge(dv_done, U)
                    psF = gate[(3 * n + 1) % 4]
                    dve.scalar_tensor_tensor(m1[:], psF[:], bias(GF, kb), isb[:], ALU.add, ALU.min)\
                        .then_inc(m1_done, 1)
                    if lag:
                        split(U - 1)
                    dve.wait_ge(m1_done, U + 1)
                    dve.wait_ge(q_done, U)
                    dve.scalar_tensor_tensor(eu[:], m1[:], 0.0, psF[:], ALU.min, ALU.subtract)\
                        .then_inc(du_done, 1)
                    dve.wait_ge(p_done, U)
                    dve.scalar_tensor_tensor(ev[:], m1[:], 0.0, isb[:], ALU.min, ALU.subtract)\
                        .then_inc(dv_done, 1)
                    dve.wait_ge(en_done, U + 1)
                    dve.wait_ge(eu_done, U + 1)
                    dve.wait_ge(scan_done, U)
                    dve.scalar_tensor_tensor(qb[:], en[:], 1.0, eu[:], ALU.min, ALU.add).then_inc(q_done, 1)
                    dve.wait_ge(ev_done, U + 1)
                    dve.scalar_tensor_tensor(pa[:], en[:], 1.0, ev[:], ALU.min, ALU.add).then_inc(p_done, 1)
                    dve.wait_ge(hp_done, U + 1)
                    dve.wait_ge(eh_done, U)
                    dve.wait_ge(sd_done, U)
                    dve.tensor_scalar(hm[:], gate[(3 * n + 2) % 4][:], bias(GH, kb), 0.0, ALU.add, ALU.min)\
                        .then_inc(hm_done, 1)
                    if kb == 0 and not (first and n == 0):
                        output(seq * CPS + n // NB - 1)
                    dve.wait_ge(r_done, U + 1)
                    dve.wait_ge(d_done, U + 1)
                    dve.tensor_tensor(pa[:], pa[:], dn[:], ALU.mult).then_inc(a_done, 1)
                    dve.wait_ge(sig_done, U + 1)
                    dve.wait_ge(hp_done, U + 1)
                    dve.wait_ge(b_done, U)
                    dve.tensor_tensor(gg[:], hp[:], sd[:], ALU.max).then_inc(g_done, 1)
                    if first and n + 2 < NB:
                        lo(n + 2)

            sequences(dve, body)
            scan(B * UPS - 1, UPS - 1)
            split(B * UPS - 1)
            output(NCH - 1)

        @block.tensor
        def _(pe):
            pe.wait_ge(small, 48)
            pe.wait_ge(prep, 2)
            pe.matmul(psY[0][:], one_row[:], b2row[:], start=True, stop=True).then_inc(b2_mm, 1)
            pe.wait_ge(prep, 11)

            def outputs(U, n, c):
                kb = n % NB
                pe.wait_ge(hi_done, U + 1)
                pe.wait_ge(lo_done, U + 1)
                if isinstance(U, int) and U < NB:
                    pe.wait_ge(w2_lo, U + 1)
                if kb == 0:
                    pe.wait_ge(y_done, c * TILES)
                for q in range(TILES):
                    sl = slice(q * P, (q + 1) * P)
                    mm = matmul_pairs(pe, psY[q][:], (hT[:, 0, sl], hT[:, 1, sl]),
                                      (w2[0][:, kb, :], w2[1][:, kb, :]), kb == 0, kb == NB - 1)
                    if kb == NB - 1 and q < TILES - 1:
                        mm.then_inc(y_mm, 1)
                mm.then_inc(out_mm, 1)

            def body(u0, seq, first):
                for n in range(UPS):
                    U, kb, j = u0 + n, n % NB, n // NB
                    if kb == 0:
                        pe.wait_ge(xT_loaded[j], (seq + 1) * 16)
                    if first and n < NB:
                        pe.wait_ge(w1_lo, n + 1)
                    for g, third, done, freed in ((0, GI, i_mm, None), (1, GF, f_mm, isb_done), (2, GH, h_mm, du_done)):
                        bank = gate[(3 * n + g) % 4]
                        if g > 0:
                            pe.wait_ge(freed, U)
                        elif not (first and n < 2):
                            pe.wait_ge(hm_done, U - 1)
                            pe.wait_ge(hp_done, U - 1)
                        cols = slice(third * z.DIN + kb * P, third * z.DIN + (kb + 1) * P)
                        for kk in range(KD):
                            mm = matmul_pairs(pe, bank[:], (w1[0][:, kk, cols], w1[1][:, kk, cols]),
                                              (xT[j][:, 0, kk, :], xT[j][:, 1, kk, :]), kk == 0, kk == KD - 1)
                        mm.then_inc(done, 1)
                    if not (first and n == 0):
                        outputs(U - 1, (n - 1) % UPS, seq * CPS + (n - 1) // NB)

            sequences(pe, body)
            outputs(B * UPS - 1, UPS - 1, NCH - 1)


def routed_sweep(nc, z, x, rgw, ruw, rdw, xs_dram, ss_dram, tok_dram, tile_expert, tile_switch,
                 ident, out):
    KD, NI, D, E, NS, T = z.KD, z.NI, z.D, z.E, z.NS, z.T
    HALF = z.I // 2
    KH = NI // 2
    PARTS = 6
    G0, U0, G1, U1, D0, D1 = range(PARTS)
    BY_POOL = (U0, D0)
    x_rows = x.rearrange("b s d -> (b s) d")
    out_rows = out.rearrange("b s d -> (b s) d")
    with ExitStack() as ctx:
        k = Kit(nc, ctx)
        raw = [k.sb(f"raw{q}", [P, 4, 512]) for q in range(PARTS)]
        whi = [k.sb(f"whi{q}", [P, 4, 512], F32R) for q in range(PARTS)]
        wlo = [k.sb(f"wlo{q}", [P, 4, 512], F32R) for q in range(PARTS)]
        xg = k.sb("xg", [P, D])
        xT = k.sb("txT", [P, 2, KD, P], F32R)
        sg = [k.sb(f"tsg{n}", [P, HALF]) for n in range(2)]
        h = [k.sb(f"th{n}", [P, HALF]) for n in range(2)]
        hT = [k.sb(f"thT{n}", [P, 2, KH, P], F32R) for n in range(2)]
        ss = k.sb("shared_and_s", [P, 2 * D])
        xr = k.sb("xr", [P, D])
        zb = k.sb("zb", [P, D])
        yo = k.sb("yo", [P, D])
        back_i = k.sb("back_i", [NS, P], I32)
        back = k.sb("back", [NS, P])
        clipped = k.sb("clipped", [P, NS])
        gather_at = k.sb("gather_at", [P, NS + 1], I32)
        scatter_at = k.sb("scatter_at", [P, NS + 1], I32)
        at_next = k.sb("at_next", [P, 1], I32)
        at_this = k.sb("at_this", [P, 1], I32)
        at_out = k.sb("at_out", [P, 1], I32)
        psG = [k.ps(f"tG{n}", [P, HALF]) for n in range(2)]
        psU = [k.ps(f"tU{n}", [P, HALF]) for n in range(2)]
        psX = k.ps("tX", [P, KD, P])
        psH = [k.ps(f"tH{n}", [P, KH, P]) for n in range(2)]
        psY = k.ps("tY", [P, D])

        raw_loaded = [k.sem(f"raw_loaded{q}") for q in range(PARTS)]
        whi_done = [k.sem(f"whi_done{q}") for q in range(PARTS)]
        wlo_done = [k.sem(f"wlo_done{q}") for q in range(PARTS)]
        used = [k.sem(f"used{q}") for q in range(PARTS)]
        settled = k.sem("settled")
        returned = k.sem("returned")
        back_done = k.sem("back_done")
        turned_table = k.sem("turned_table")
        table = k.sem("table")
        at_done = k.sem("at_done")
        at_out_done = k.sem("at_out_done")
        xg_loaded = k.sem("xg_loaded")
        ss_loaded = k.sem("ss_loaded")
        xr_loaded = k.sem("xr_loaded")
        out_stored = k.sem("out_stored")
        turned_x = k.sem("turned_x")
        xhi = k.sem("txhi")
        xlo = k.sem("txlo")
        sg_done = [k.sem(f"tsg_done{n}") for n in range(2)]
        h_done = [k.sem(f"th_done{n}") for n in range(2)]
        turned_h = [k.sem(f"turned_h{n}") for n in range(2)]
        hhi = [k.sem(f"thhi{n}") for n in range(2)]
        hlo = [k.sem(f"thlo{n}") for n in range(2)]
        z_done = k.sem("z_done")
        zs_done = k.sem("zs_done")
        zm_done = k.sem("zm_done")
        yo_done = k.sem("yo_done")
        block = ctx.enter_context(nc.Block())

        def tiles(eng, body, switches=True):
            with eng.Fori(0, NS) as t:
                e = eng.value_load(tile_expert[0:1, bass.ds(t, 1)], min_val=0, max_val=E)
                if switches:
                    s = eng.value_load(tile_switch[0:1, bass.ds(t, 1)], min_val=0, max_val=1)
                with eng.If(e < E):
                    if switches:
                        with eng.If(s > 0):
                            body(t, e, True)
                        with eng.Else():
                            body(t, e, False)
                    else:
                        body(t, e, False)

        def part(q, e):
            if q < D0:
                w = (rgw, ruw)[q % 2][e].rearrange("(k p) i -> p k i", p=P)
                return w[:, :, (q // 2) * HALF:(q // 2 + 1) * HALF]
            return rdw[e].rearrange("(k p) d -> p k d", p=P)[:, (q - D0) * KH:(q - D0 + 1) * KH, :]

        @block.sync
        def _(sp):
            sp.dma_start(back_i[:], tok_dram.rearrange("(s p) a -> s (p a)", p=P)).then_inc(returned, 16)
            with sp.Fori(0, E) as e:
                for q in range(PARTS):
                    sp.wait_ge(wlo_done[q], e)
                    sp.dma_start(raw[q][:], part(q, e)).then_inc(raw_loaded[q], 16)

        def split_hi(act, q, e, t):
            act.wait_ge(raw_loaded[q], (e + 1) * 16)
            if t is not None:
                act.wait_ge(used[q], t + 1)
            act.activation(whi[q][:], raw[q][:], ACT.Copy).then_inc(whi_done[q], 1)

        def split_lo(eng, q, e):
            eng.wait_ge(whi_done[q], e + 1)
            eng.tensor_tensor(wlo[q][:], raw[q][:], whi[q][:], ALU.subtract).then_inc(wlo_done[q], 1)

        @block.gpsimd
        def _(pool):
            def fetch(dst, src, at, done):
                pool.indirect_dma_start(out=dst, out_offset=None, in_=src,
                                        in_offset=bass.IndirectOffsetOnAxis(ap=at, axis=0)).then_inc(done, 16)

            def scatter(t):
                pool.wait_ge(out_stored, t * 16)
                settle(pool, settled)
                pool.tensor_copy(at_out[:], scatter_at[:, bass.ds(t, 1)]).then_inc(at_out_done, 1)
                pool.wait_ge(at_out_done, t + 1)
                pool.wait_ge(yo_done, t + 1)
                settle(pool, settled)
                pool.indirect_dma_start(out=out_rows, out_offset=bass.IndirectOffsetOnAxis(ap=at_out[:], axis=0),
                                        in_=yo[:], in_offset=None, bounds_check=T - 1,
                                        oob_is_err=False).then_inc(out_stored, 16)

            pool.memset(yo[:], 0.0).then_inc(yo_done, 1)
            pool.wait_ge(table, 5)
            pool.tensor_copy(at_next[:], gather_at[:, 0:1]).then_inc(at_done, 1)
            pool.wait_ge(at_done, 1)
            fetch(xg[:], xs_dram, at_next[:], xg_loaded)
            for q in BY_POOL:
                split_lo(pool, q, 0)

            def body(t, e, switch):
                pool.wait_ge(xg_loaded, (t + 1) * 16)
                settle(pool, settled)
                pool.tensor_copy(at_next[:], gather_at[:, bass.ds(t + 1, 1)]).then_inc(at_done, 1)
                pool.wait_ge(at_done, t * 2 + 2)
                pool.wait_ge(turned_x, t + 1)
                settle(pool, settled)
                fetch(xg[:], xs_dram, at_next[:], xg_loaded)
                scatter(t)
                pool.wait_ge(ss_loaded, t * 16)
                pool.wait_ge(xr_loaded, t * 16)
                settle(pool, settled)
                pool.tensor_copy(at_this[:], gather_at[:, bass.ds(t, 1)]).then_inc(at_done, 1)
                pool.wait_ge(at_done, t * 2 + 3)
                settle(pool, settled)
                fetch(ss[:], ss_dram, at_this[:], ss_loaded)
                fetch(xr[:], x_rows, at_this[:], xr_loaded)
                if switch:
                    split_lo(pool, U0, e + 1)
                    split_lo(pool, D0, e + 1)

            tiles(pool, body)
            total = pool.value_load(tile_expert[0:1, NS + 1:NS + 2], min_val=1, max_val=NS)
            scatter(total)
            pool.wait_ge(out_stored, total * 16 + 16)
            settle(pool, settled)
            pool.memset(at_out[:], 0).then_inc(at_done, 1)

        @block.scalar
        def _(act):
            def x_hi(t):
                act.wait_ge(turned_x, t + 1)
                act.wait_ge(used[U1], t)
                act.activation(xT[:, 0], psX[:], ACT.Copy).then_inc(xhi, 1)

            x_hi(0)
            for q in range(PARTS):
                split_hi(act, q, 0, None)

            def body(t, e, switch):
                def silu(n):
                    act.wait_ge(used[(G0, G1)[n]], t + 1)
                    act.wait_ge(h_done[n], t)
                    act.activation(sg[n][:], psG[n][:], ACT.Silu).then_inc(sg_done[n], 1)

                def h_hi(n):
                    act.wait_ge(turned_h[n], t + 1)
                    act.wait_ge(used[(D0, D1)[n]], t)
                    act.activation(hT[n][:, 0], psH[n][:], ACT.Copy).then_inc(hhi[n], 1)

                def hi(q):
                    if switch:
                        split_hi(act, q, e + 1, t)

                silu(0)
                hi(G0)
                hi(U0)
                silu(1)
                h_hi(0)
                hi(G1)
                hi(U1)
                h_hi(1)
                x_hi(t + 1)
                hi(D0)
                act.wait_ge(z_done, t + 1)
                act.activation(zb[:], zb[:], ACT.Silu).then_inc(zs_done, 1)
                hi(D1)

            tiles(act, body)

        @block.vector
        def _(dve):
            def lo(q, e):
                if q not in BY_POOL:
                    split_lo(dve, q, e)

            def x_lo(t):
                dve.wait_ge(xhi, t + 1)
                dve.tensor_tensor(xT[:, 1], psX[:], xT[:, 0], ALU.subtract).then_inc(xlo, 1)

            dve.wait_ge(returned, 16)
            dve.tensor_copy(back[:], back_i[:]).then_inc(back_done, 1)
            dve.wait_ge(turned_table, 1)
            dve.tensor_copy(scatter_at[:, 1:NS + 1], psY[:, 0:NS]).then_inc(table, 1)
            dve.tensor_scalar(clipped[:], psY[:, 0:NS], float(T - 1), None, ALU.min).then_inc(table, 1)
            dve.memset(scatter_at[:, 0:1], T).then_inc(table, 1)
            dve.memset(gather_at[:, NS:NS + 1], 0).then_inc(table, 1)
            dve.wait_ge(table, 4)
            dve.tensor_copy(gather_at[:, 0:NS], clipped[:]).then_inc(table, 1)
            x_lo(0)
            for q in range(PARTS):
                lo(q, 0)

            def body(t, e, switch):
                def h_mul(n):
                    dve.wait_ge(sg_done[n], t + 1)
                    dve.wait_ge(used[(U0, U1)[n]], t + 1)
                    dve.wait_ge(turned_h[n], t)
                    dve.tensor_tensor(h[n][:], sg[n][:], psU[n][:], ALU.mult).then_inc(h_done[n], 1)

                def h_lo(n):
                    dve.wait_ge(hhi[n], t + 1)
                    dve.tensor_tensor(hT[n][:, 1], psH[n][:], hT[n][:, 0], ALU.subtract).then_inc(hlo[n], 1)

                def nxt(q):
                    if switch:
                        lo(q, e + 1)

                h_mul(0)
                nxt(G0)
                h_lo(0)
                h_mul(1)
                nxt(G1)
                h_lo(1)
                x_lo(t + 1)
                nxt(U1)
                dve.wait_ge(used[D1], t + 1)
                dve.wait_ge(ss_loaded, (t + 1) * 16)
                dve.wait_ge(zm_done, t)
                dve.tensor_tensor(zb[:], psY[:], ss[:, 0:D], ALU.add).then_inc(z_done, 1)
                dve.wait_ge(zs_done, t + 1)
                dve.wait_ge(out_stored, (t + 1) * 16)
                dve.tensor_tensor(yo[:], zb[:], ss[:, D:2 * D], ALU.mult).then_inc(zm_done, 1)
                dve.wait_ge(zm_done, t + 1)
                dve.wait_ge(xr_loaded, (t + 1) * 16)
                dve.tensor_tensor(yo[:], yo[:], xr[:], ALU.add).then_inc(yo_done, 1)
                nxt(D1)

            tiles(dve, body)

        @block.tensor
        def _(pe):
            def turn_x(t):
                pe.wait_ge(xg_loaded, (t + 1) * 16)
                pe.wait_ge(xlo, t)
                for kb in range(KD):
                    mm = pe.transpose(psX[:, kb, :], xg[:, kb * P:(kb + 1) * P], ident[:])
                mm.then_inc(turned_x, 1)

            pe.wait_ge(back_done, 1)
            pe.transpose(psY[:, 0:NS], back[:], ident[0:NS, 0:NS]).then_inc(turned_table, 1)
            pe.wait_ge(table, 2)
            turn_x(0)

            def body(t, e, switch):
                def up(q, bank, freed):
                    pe.wait_ge(wlo_done[q], e + 1)
                    pe.wait_ge(freed, t)
                    for kb in range(KD):
                        mm = matmul_pairs(pe, bank[:], (xT[:, 0, kb, :], xT[:, 1, kb, :]),
                                          (whi[q][:, kb, :], wlo[q][:, kb, :]), kb == 0, kb == KD - 1)
                    mm.then_inc(used[q], 1)

                def turn_h(n):
                    pe.wait_ge(h_done[n], t + 1)
                    pe.wait_ge(hlo[n], t)
                    for kb in range(KH):
                        mm = pe.transpose(psH[n][:, kb, :], h[n][:, kb * P:(kb + 1) * P], ident[:])
                    mm.then_inc(turned_h[n], 1)

                def down(n, blocks):
                    q = (D0, D1)[n]
                    if blocks[0] == 0:
                        pe.wait_ge(wlo_done[q], e + 1)
                        pe.wait_ge(hlo[n], t + 1)
                        if n == 0:
                            pe.wait_ge(z_done, t)
                    for kb in blocks:
                        mm = matmul_pairs(pe, psY[:], (hT[n][:, 0, kb, :], hT[n][:, 1, kb, :]),
                                          (whi[q][:, kb, :], wlo[q][:, kb, :]),
                                          n == 0 and kb == 0, n == 1 and kb == KH - 1)
                    if blocks[-1] == KH - 1:
                        mm.then_inc(used[q], 1)

                pe.wait_ge(xlo, t + 1)
                up(G0, psG[0], sg_done[0])
                up(U0, psU[0], h_done[0])
                up(G1, psG[1], sg_done[1])
                turn_h(0)
                up(U1, psU[1], h_done[1])
                turn_x(t + 1)
                down(0, range(0, KH // 2))
                turn_h(1)
                down(0, range(KH // 2, KH))
                down(1, range(KH))

            tiles(pe, body, switches=False)


def moe_recurrent_kernel(nc, x, W1, b1, W2, b2, init_h, gate_w, sgw, suw, sdw, rgw, ruw, rdw, out):
    z = Shapes(x, W1, gate_w, sgw)
    xT_dram = nc.dram_tensor("xT_dram", [z.NCH, P, 2, z.KD, CHUNK], F32).ap()
    xs_dram = nc.dram_tensor("xs_dram", [z.T, z.D], F32).ap()
    ss_dram = nc.dram_tensor("ss_dram", [z.T, 2 * z.D], F32).ap()
    tok_dram = nc.dram_tensor("tok_dram", [z.NS * P, 1], I32).ap()
    with ExitStack() as ctx:
        k = Kit(nc, ctx)
        ident = k.sb("ident", [P, P])
        slot = k.sb("slot", [P, z.NT], I32)
        token = k.sb("token", [P, z.NT], I32)
        tile_expert = k.sb("tile_expert", [1, z.NS + 2], I32)
        tile_switch = k.sb("tile_switch", [1, z.NS], I32)
        with nc.sbuf_tensor("onehot", [P, z.NT, z.E], BF16) as onehot:
            shared_sweep(nc, z, x, gate_w, sgw, suw, sdw, xT_dram, xs_dram, ss_dram, onehot, ident)
            routing(nc, z, onehot, tok_dram, slot, token, tile_expert, tile_switch)
        recurrence_sweep(nc, z, xT_dram, W1, b1, W2, b2, init_h, ss_dram, slot, token, tok_dram)
        routed_sweep(nc, z, x, rgw, ruw, rdw, xs_dram, ss_dram, tok_dram, tile_expert, tile_switch,
                     ident, out)


_INS = ["L0_attn_x", "L0_attn_W1", "L0_attn_b1", "L0_attn_W2", "L0_attn_b2", "L0_attn_init_h",
        "L0_ffn_gate_w", "L0_ffn_shared_gate_w", "L0_ffn_shared_up_w", "L0_ffn_shared_down_w",
        "L0_ffn_routed_gate_w", "L0_ffn_routed_up_w", "L0_ffn_routed_down_w"]


def kernel(**inputs):
    import numpy as np
    import concourse.bacc as bacc
    from concourse.bass_utils import run_bass_kernel_spmd

    nc = bacc.Bacc("TRN2", target_bir_lowering=False, num_devices=1)
    arrays, args = {}, []
    for name in _INS:
        a = np.ascontiguousarray(inputs[name])
        arrays[f"in_{name}"] = a
        args.append(nc.dram_tensor(f"in_{name}", a.shape, mybir.dt.from_np(a.dtype), kind="ExternalInput").ap())
    args.append(nc.dram_tensor("out_0", inputs["L0_attn_x"].shape, F32, kind="ExternalOutput").ap())
    moe_recurrent_kernel(nc, *args)
    r = run_bass_kernel_spmd(nc, [arrays], core_ids=[0])
    return r.results[0]["out_0"]
```

```python
from contextlib import ExitStack

import concourse.bass as bass
from concourse import mybir

ALU = mybir.AluOpType
ACT = mybir.ActivationFunctionType
F32 = mybir.dt.float32
F32R = mybir.dt.float32r
BF16 = mybir.dt.bfloat16
I32 = mybir.dt.int32
U32 = mybir.dt.uint32
AX_X = mybir.AxisListType.X
P = 128
CHUNK = 512
TILES = CHUNK // P
EPS = 1e-5
GROUP = 8


class Shapes:

    def __init__(self, x, W1, gate_w, sgw):
        self.B, self.S, self.D = x.shape
        self.T = self.B * self.S
        self.KD = self.D // P
        self.DIN = W1.shape[1] // 3
        self.NB = self.DIN // P
        self.E = gate_w.shape[1]
        self.I = sgw.shape[1]
        self.NI = self.I // P
        self.NCH = self.T // CHUNK
        self.NT = self.T // P
        self.NS = self.NT + self.E
        self.GROUPS = -(-(self.NS - 1) // GROUP)
        self.PLACES = 1 + self.GROUPS * GROUP


class Kit:

    def __init__(self, nc, ctx):
        self.nc, self.ctx, self.sems = nc, ctx, []
        ctx.callback(self.clear)

    def clear(self):
        if self.sems:
            self.nc.clear_and_free_semaphores(self.sems)
            self.nc.all_engine_barrier()

    def sb(self, name, shape, dt=F32):
        return self.ctx.enter_context(self.nc.sbuf_tensor(name, shape, dt))

    def ps(self, name, shape, dt=F32):
        return self.ctx.enter_context(self.nc.psum_tensor(name, shape, dt))

    def sem(self, name):
        self.sems.append(self.nc.alloc_semaphore(name))
        return self.sems[-1]


def settle(eng, settled):
    eng.sem_inc(settled, 1)


def matmul_pairs(pe, out, w, x, start, stop):
    pe.matmul(out, w[0], x[0], start=start, stop=False)
    pe.matmul(out, w[0], x[1], start=False, stop=False)
    return pe.matmul(out, w[1], x[0], start=False, stop=stop)


def round_hi(act, hi, raw, done):
    act.activation(hi, raw, ACT.Copy).then_inc(done, 1)


def leave_lo(eng, lo, raw, hi, done):
    eng.tensor_tensor(lo, raw, hi, ALU.subtract).then_inc(done, 1)


def at_least(eng, sem, value):
    if not isinstance(value, int) or value > 0:
        eng.wait_ge(sem, value)


def shared_sweep(nc, z, x, gate_w, sgw, suw, sdw, xT, xT_dram, xs_dram, ss_dram, onehot, ident, tok_dram,
                 slot, token, first_tile, b1, b1s, init_h, i0):
    NT, NS, T = z.NT, z.NS, z.T
    N = NT * z.E
    KD, NI, E, D, I, NCH = z.KD, z.NI, z.E, z.D, z.I, z.NCH
    x_v = x.rearrange("b s d -> (b s) d").rearrange("(c q p) d -> c p q d", q=TILES, p=P)
    xs_v = xs_dram.rearrange("(c q p) d -> c p q d", q=TILES, p=P)
    ss_t = ss_dram.rearrange("(t p) d -> t p d", p=P)
    with ExitStack() as ctx:
        k = Kit(nc, ctx)
        gup = [k.sb(f"gu_{h}", [P, 2, KD, I], F32R) for h in ("hi", "lo")]
        dnp = [k.sb(f"dn_{h}", [P, NI, D], F32R) for h in ("hi", "lo")]
        rt = k.sb("router", [P, KD, 2, E], F32R)
        QC = I // TILES
        y = k.sb("y_sb", [P, 2, D])
        assert 2 * D == KD * QC
        raw = [y[:].rearrange("p q d -> p (q d)"), k.sb("raw_weights", [P, KD * QC])[:]]
        order, parts = [], {}

        def part(key, hi_lo, src):
            stage = raw[len(order) % 2][:, 0:src.shape[1] * src.shape[2]]
            parts[key] = (hi_lo, src, stage.rearrange("p (a b) -> p a b", a=src.shape[1]))
            order.append(key)

        def down_part(n):
            ks = slice(n * NI // TILES, (n + 1) * NI // TILES)
            part(("down", n), [w[:, ks, :] for w in dnp], sdw.rearrange("(k p) d -> p k d", p=P)[:, ks, :])

        part("router", [rt[:, :, n, :] for n in range(2)], gate_w.rearrange("(k p) e -> p k e", p=P))
        for n in range(TILES):
            cols = slice(n * QC, (n + 1) * QC)
            for m, w in enumerate((sgw, suw)):
                part((m, n), [g[:, m, :, cols] for g in gup], w.rearrange("(k p) i -> p k i", p=P)[:, :, cols])
            if n > 0:
                down_part(n - 1)
        down_part(TILES - 1)

        x_in = k.sb("x_in", [P, 2, TILES, D])
        xn = k.sb("xn", [P, TILES, D])
        stats = k.sb("stats", [P, TILES, 6])
        mv = k.sb("mv", [P, 2, TILES, 2])
        std = k.sb("std", [P, TILES])
        r0 = k.sb("r0", [P, TILES])
        vr = k.sb("vr", [P, TILES])
        vrr = k.sb("vrr", [P, TILES])
        half = k.sb("half", [P, TILES])
        rstd = k.sb("rstd", [P, 2, TILES])
        rs = k.sb("rs", [P, TILES])
        logits = k.sb("logits", [P, TILES, E])
        top = k.sb("top", [P, TILES, 8])
        topi = k.sb("topi", [P, TILES, 8], U32)
        topf = k.sb("topf", [P, TILES])
        score = k.sb("score", [P, TILES])
        iota_e = k.sb("iota_e", [P, E])
        TB = CHUNK // E
        pieces = [(t, min(t + TB, NT)) for t in range(0, NT, TB)]
        assert len(pieces) <= 4 and N <= TILES * D
        flat = lambda a: a.rearrange("p q d -> p (q d)")[:, 0:N]
        tot = flat(x_in[:, 0]).rearrange("p (e t) -> p e t", e=E)
        incl = flat(x_in[:, 1]).rearrange("p (e t) -> p e t", e=E)
        base = flat(xn[:]).rearrange("p (e t) -> p e t", e=E)
        cand = flat(x_in[:, 0]).rearrange("p (t e) -> p t e", e=E)
        before = k.sb("before", [P, P], BF16)
        ones = k.sb("ones", [P, P], BF16)
        count = k.sb("count", [P, E])
        count_i = k.sb("count_i", [P, E], I32)
        tiles_i = k.sb("tiles_i", [P, E], I32)
        tiles_f = k.sb("tiles_f", [P, E])
        first_incl = k.sb("first_incl", [P, E])
        off = k.sb("off", [P, E])
        slot_f = k.sb("slot_f", [P, NT])
        fill = k.sb("fill", [NS, P], I32)
        eps = k.sb("eps", [P, 1])
        h = k.sb("h_act", [P, 2, CHUNK])
        by_expert = h[0:2 * E, 0]
        hT = k.sb("hT", [P, 2, NI, CHUNK], F32R)

        psG = [k.ps(f"psG{i}", [P, CHUNK]) for i in range(2)]
        psU = [k.ps(f"psU{i}", [P, CHUNK]) for i in range(2)]
        psY = [k.ps(f"psY{i}", [P, D]) for i in range(2)]
        psT = k.ps("psT", [P, KD, P])
        psL = k.ps("psL", [2 * E, CHUNK])
        by_token = psT[:].rearrange("p k t -> p (k t)")[:, 0:TILES * 2 * E].rearrange("p (q e) -> p q e", q=TILES)

        def turned(c, q):
            if isinstance(c, int) and c == 0 and q > 0:
                return (psG[0], psG[1], psU[0])[q - 1][:].rearrange("p (k t) -> p k t", k=KD)
            return psT[:]

        x_loaded = [k.sem(f"x_loaded{j}") for j in range(2)]
        xs_stored = k.sem("xs_stored")
        xT_stored = [k.sem(f"xT_stored{j}") for j in range(2)]
        y_stored = [k.sem(f"y_stored{j}") for j in range(2)]
        stats_done = k.sem("stats_done")
        mv_done = k.sem("mv_done")
        std_done = k.sem("std_done")
        r0_done = k.sem("r0_done")
        newton = k.sem("newton")
        xn_done = k.sem("xn_done")
        xpose_done = k.sem("xpose_done")
        xhi_done = k.sem("xhi_done")
        xlo_done = k.sem("xlo_done")
        logits_mm = k.sem("logits_mm")
        by_expert_done = k.sem("by_expert_done")
        by_token_done = k.sem("by_token_done")
        logits_done = k.sem("logits_done")
        top_done = k.sem("top_done")
        topi_done = k.sem("topi_done")
        topf_done = k.sem("topf_done")
        onehot_done = k.sem("onehot_done")
        score_done = k.sem("score_done")
        xs_done = k.sem("xs_done")
        const_done = k.sem("const_done")
        settled = k.sem("settled1")
        rs_done = k.sem("rs_done")
        sort_const = k.sem("sort_const")
        filled = k.sem("filled")
        small = k.sem("small_loaded")
        piece_mm = k.sem("piece_mm")
        piece_read = k.sem("piece_read")
        sort_step = k.sem("sort_step")
        w_loaded = {key: k.sem(f"w_loaded{n}") for n, key in enumerate(order)}
        w_hi = k.sem("w_hi")
        w_lo = k.sem("w_lo")
        g_mm = k.sem("g_mm")
        u_mm = k.sem("u_mm")
        sg_done = k.sem("sg_done")
        h_done = k.sem("h_done")
        hhi_done = k.sem("hhi_done")
        hlo_done = k.sem("hlo_done")
        y_mm = k.sem("y_mm")
        y_copied = k.sem("y_copied")
        block = ctx.enter_context(nc.Block())

        def chunks(eng, one):
            for j in range(2):
                one(j, j, 0, True, NCH > 2)
            if NCH > 4:
                with eng.Fori(1, NCH // 2 - 1) as it:
                    for j in range(2):
                        one(it * 2 + j, j, it, True, True)
            it = NCH // 2 - 1
            for j in range(2):
                one(it * 2 + j, j, it, j == 0, False)

        def nxt(c, j, it):
            return c + 1, 1 - j, it + j

        def nxt2(c, j, it):
            return c + 2, j, it + 1

        def weights(c, b, split):
            if isinstance(c, int) and c == 0:
                if b % 2 == 0 and b + 2 < NI:
                    split((0, b // 2 + 1))
                    split((1, b // 2 + 1))
                elif b % 2 == 1:
                    split(("down", b // 2))

        @block.sync
        def _(sp):
            def load(c, j, it):
                at_least(sp, xs_stored, (c - 1) * 16)
                sp.dma_start(x_in[:, j], x_v[c]).then_inc(x_loaded[j], 16)

            def store_xT(c, j, it):
                sp.wait_ge(xlo_done, (c + 1) * TILES)
                sp.dma_start(xT_dram[c], xT[j][:].bitcast(F32)).then_inc(xT_stored[j], 16)

            def store_xs(c, j, it):
                sp.wait_ge(xs_done, (c + 1) * TILES)
                sp.dma_start(xs_v[c], x_in[:, j]).then_inc(xs_stored, 16)

            def one(c, j, it, more, more2):
                if more2 and not (isinstance(c, int) and c == 0):
                    load(*nxt2(c, j, it))
                if more:
                    store_xT(*nxt(c, j, it))
                for q in range(TILES):
                    if q == TILES // 2 and more:
                        store_xs(*nxt(c, j, it))
                    sp.wait_ge(y_copied, c * TILES + q + 1)
                    sp.dma_start(ss_t[c * TILES + q][:, 0:D], y[:, q % 2]).then_inc(y_stored[q % 2], 16)

            load(0, 0, 0)
            for n, key in enumerate(order):
                at_least(sp, w_lo, n - 1)
                sp.dma_start(parts[key][2], parts[key][1]).then_inc(w_loaded[key], 16)
                if n == 1:
                    load(1, 1, 0)
                elif key == (1, TILES - 1):
                    store_xT(0, 0, 0)
                    store_xs(0, 0, 0)
                    if NCH > 2:
                        load(2, 0, 1)
            sp.wait_ge(sort_const, 4)
            sp.dma_start(tok_dram.rearrange("(s p) a -> s (p a)", p=P), fill[:]).then_inc(filled, 16)
            sp.dma_start(b1s[:], b1.rearrange("(g p) -> p g", p=P),
                         allow_slow_non_contiguous=True).then_inc(small, 16)
            sp.dma_start(i0[:], init_h.rearrange("(g p) -> p g", p=P),
                         allow_slow_non_contiguous=True).then_inc(small, 16)
            chunks(sp, one)
            sp.wait_ge(filled, 16)
            sp.wait_ge(small, 32)
            sp.wait_ge(xs_stored, 16 * NCH)
            for j in range(2):
                sp.wait_ge(xT_stored[j], 16 * (NCH // 2))
                sp.wait_ge(y_stored[j], 16 * (NCH * TILES // 2))

        @block.gpsimd
        def _(pool):
            pool.iota(iota_e[:], [[1, E]], base=0, channel_multiplier=0,
                      allow_small_or_imprecise_dtypes=True).then_inc(const_done, 1)
            pool.memset(eps[:], EPS).then_inc(const_done, 1)
            pool.memset(ident[:], 0.0).then_inc(const_done, 1)
            pool.wait_ge(const_done, 3)
            pool.affine_select(out=ident[:], in_=ident[:], compare_op=ALU.not_equal, fill=1.0, base=0,
                               pattern=[[-1, P]], channel_multiplier=1).then_inc(const_done, 1)

            def prep(c, j, it):
                pool.wait_ge(r0_done, c + 1)
                settle(pool, settled)
                pool.tensor_scalar(vr[:], mv[:, j, :, 1], EPS, None, ALU.add).then_inc(newton, 1)
                pool.wait_ge(newton, c * 5 + 1)
                pool.tensor_tensor(vrr[:], vr[:], r0[:], ALU.mult).then_inc(newton, 1)
                pool.wait_ge(newton, c * 5 + 2)
                pool.tensor_tensor(half[:], vrr[:], r0[:], ALU.mult).then_inc(newton, 1)
                pool.wait_ge(newton, c * 5 + 3)
                settle(pool, settled)
                pool.tensor_scalar(vr[:], half[:], -0.5, 1.5, ALU.mult, ALU.add).then_inc(newton, 1)
                pool.wait_ge(newton, c * 5 + 4)
                at_least(pool, xn_done, (c - 1) * TILES)
                at_least(pool, rs_done, c - 1)
                pool.tensor_tensor(rstd[:, j], vr[:], r0[:], ALU.mult).then_inc(newton, 1)

            def scale(c, j, it):
                pool.wait_ge(score_done, c + 1)
                pool.wait_ge(newton, c * 5 + 5)
                at_least(pool, xs_done, c * TILES)
                pool.tensor_tensor(rs[:], rstd[:, j], score[:], ALU.mult).then_inc(rs_done, 1)
                pool.wait_ge(rs_done, c + 1)
                pool.wait_ge(xn_done, (c + 1) * TILES)
                settle(pool, settled)
                for q in range(TILES):
                    pool.tensor_scalar(x_in[:, j, q], x_in[:, j, q], mv[:, j, q, 0:1], rs[:, q:q + 1],
                                       ALU.subtract, ALU.mult).then_inc(xs_done, 1)

            def one(c, j, it, more, more2):
                if more2:
                    prep(*nxt2(c, j, it))
                if more:
                    scale(*nxt(c, j, it))

            prep(0, 0, 0)
            pool.memset(before[:], 1.0).then_inc(sort_const, 1)
            pool.memset(ones[:], 1.0).then_inc(sort_const, 1)
            pool.memset(fill[:], T).then_inc(sort_const, 1)
            pool.iota(token[:], [[P, NT]], base=0, channel_multiplier=1).then_inc(sort_const, 1)
            pool.wait_ge(sort_const, 4)
            pool.affine_select(out=before[:], in_=before[:], compare_op=ALU.is_gt, fill=0.0, base=0,
                               pattern=[[1, P]], channel_multiplier=-1).then_inc(sort_const, 1)
            prep(1, 1, 0)
            scale(0, 0, 0)
            chunks(pool, one)

        @block.scalar
        def _(act):
            act.wait_ge(const_done, 4)

            def hi(key):
                act.wait_ge(w_loaded[key], 16)
                round_hi(act, parts[key][0][0], parts[key][2], w_hi)

            def roots(c, j, it):
                act.wait_ge(mv_done, (c + 1) * TILES)
                at_least(act, r0_done, c)
                act.activation(std[:], mv[:, j, :, 1], ACT.Sqrt, bias=eps[:, 0:1]).then_inc(std_done, 1)

            def x_hi(c, j, it, q):
                act.wait_ge(xpose_done, c * TILES + q + 1)
                if q == 0:
                    at_least(act, xT_stored[j], it * 16)
                    at_least(act, u_mm, (c - 1) * NI)
                act.activation(xT[j][:, 0, :, q * P:(q + 1) * P], turned(c, q), ACT.Copy).then_inc(xhi_done, 1)

            def scores(c, j, it):
                act.wait_ge(top_done, (c + 1) * TILES)
                at_least(act, rs_done, c)
                act.activation(score[:], top[:, :, 0], ACT.Sigmoid).then_inc(score_done, 1)

            def h_hi(c, b):
                act.wait_ge(h_done, c * NI + b + 1)
                if b == 0:
                    at_least(act, y_mm, c * TILES)
                act.activation(hT[:, 0, b], h[:, b % 2], ACT.Copy).then_inc(hhi_done, 1)

            def one(c, j, it, more, more2):
                for b in range(NI):
                    act.wait_ge(g_mm, c * NI + b + 1)
                    at_least(act, hhi_done, c * NI + b - 1)
                    at_least(act, hlo_done, c * NI + b - 1)
                    act.activation(h[:, b % 2], psG[b % 2][:], ACT.Silu).then_inc(sg_done, 1)
                    if b >= 1:
                        h_hi(c, b - 1)
                    if more and b % 2 == 0:
                        x_hi(*nxt(c, j, it), b // 2)
                    weights(c, b, hi)
                h_hi(c, NI - 1)
                if more2:
                    roots(*nxt2(c, j, it))
                for q in range(TILES):
                    act.wait_ge(y_mm, c * TILES + q + 1)
                    at_least(act, y_stored[q % 2], (c * (TILES // 2) + q // 2) * 16)
                    act.activation(y[:, q % 2], psY[q % 2][:], ACT.Copy).then_inc(y_copied, 1)
                    if more and q == 0:
                        scores(*nxt(c, j, it))

            roots(0, 0, 0)
            hi("router")
            for q in range(TILES):
                x_hi(0, 0, 0, q)
            hi((0, 0))
            hi((1, 0))
            roots(1, 1, 0)
            scores(0, 0, 0)
            chunks(act, one)

        @block.vector
        def _(dve):
            dve.wait_ge(const_done, 4)

            def lo(key):
                dve.wait_ge(w_hi, order.index(key) + 1)
                (hi_part, lo_part), _, raw_part = parts[key]
                leave_lo(dve, lo_part, raw_part, hi_part, w_lo)

            def stats_of(c, j, it, q):
                if q == 0:
                    dve.wait_ge(x_loaded[j], (it + 1) * 16)
                    at_least(dve, mv_done, c * TILES)
                dve.bn_stats(stats[:, q], x_in[:, j, q]).then_inc(stats_done, 1)

            def moments(c, j, it):
                dve.wait_ge(stats_done, (c + 1) * TILES)
                at_least(dve, xs_done, (c - 1) * TILES)
                at_least(dve, xn_done, (c - 1) * TILES)
                settle(dve, settled)
                for q in range(TILES):
                    dve.bn_aggr(mv[:, j, q], stats[:, q]).then_inc(mv_done, 1)

            def normalise(c, j, it):
                dve.wait_ge(std_done, c + 1)
                at_least(dve, newton, c * 5)
                dve.reciprocal(r0[:], std[:]).then_inc(r0_done, 1)
                dve.wait_ge(newton, c * 5 + 5)
                at_least(dve, xpose_done, c * TILES)
                for q in range(TILES):
                    dve.tensor_scalar(xn[:, q], x_in[:, j, q], mv[:, j, q, 0:1], rstd[:, j, q:q + 1],
                                      ALU.subtract, ALU.mult).then_inc(xn_done, 1)

            def x_lo(c, j, it, q):
                dve.wait_ge(xhi_done, c * TILES + q + 1)
                sl = slice(q * P, (q + 1) * P)
                dve.tensor_tensor(xT[j][:, 1, :, sl], turned(c, q), xT[j][:, 0, :, sl], ALU.subtract)\
                    .then_inc(xlo_done, 1)

            def experts_out(c, j, it):
                dve.wait_ge(logits_mm, c + 1)
                at_least(dve, hhi_done, c * NI - 1)
                at_least(dve, hlo_done, c * NI - 1)
                dve.tensor_copy(by_expert, psL[:]).then_inc(by_expert_done, 1)

            def route(c, j, it):
                dve.wait_ge(by_token_done, c + 1)
                at_least(dve, topi_done, c * TILES)
                dve.tensor_reduce(logits[:], by_token.rearrange("p q (h e) -> p q e h", h=2), AX_X, ALU.add)\
                    .then_inc(logits_done, 1)
                dve.wait_ge(logits_done, c + 1)
                at_least(dve, score_done, c)
                settle(dve, settled)
                for q in range(TILES):
                    dve.max(top[:, q], logits[:, q]).then_inc(top_done, 1)
                dve.wait_ge(top_done, (c + 1) * TILES)
                at_least(dve, topf_done, c)
                settle(dve, settled)
                for q in range(TILES):
                    dve.max_index(topi[:, q], top[:, q], logits[:, q]).then_inc(topi_done, 1)
                dve.wait_ge(topi_done, (c + 1) * TILES)
                at_least(dve, onehot_done, c * TILES)
                dve.tensor_copy(topf[:], topi[:, :, 0]).then_inc(topf_done, 1)
                dve.wait_ge(topf_done, c + 1)
                for q in range(TILES):
                    dve.tensor_scalar(onehot[:, bass.ds(c * TILES + q, 1), :].rearrange("p a e -> p (a e)"),
                                      iota_e[:], topf[:, q:q + 1], None, ALU.is_equal).then_inc(onehot_done, 1)

            def h_mul(c, b):
                dve.wait_ge(sg_done, c * NI + b + 1)
                dve.wait_ge(u_mm, c * NI + b + 1)
                dve.tensor_tensor(h[:, b % 2], h[:, b % 2], psU[b % 2][:], ALU.mult).then_inc(h_done, 1)

            def h_lo(c, b):
                dve.wait_ge(hhi_done, c * NI + b + 1)
                dve.tensor_tensor(hT[:, 1, b], h[:, b % 2], hT[:, 0, b], ALU.subtract).then_inc(hlo_done, 1)

            steps = [0]

            def link(ins):
                steps[0] += 1
                ins.then_inc(sort_step, 1)
                dve.wait_ge(sort_step, steps[0])

            def counts(n):
                t0, t1 = pieces[n]
                dve.wait_ge(piece_mm, n + 1)
                dve.tensor_copy(tot[:, :, t0:t1], psY[n % 2][:, 0:(t1 - t0) * E].rearrange("p (t e) -> p e t", e=E))\
                    .then_inc(piece_read, 1)

            def sort(b):
                if b == 0:
                    dve.wait_ge(xs_stored, 16 * NCH)
                elif b in (1, 2):
                    for n in range(2 * b - 2, min(2 * b, len(pieces))):
                        counts(n)
                elif b == 3:
                    dve.wait_ge(piece_read, len(pieces))
                    fl = lambda a: a.rearrange("p e t -> p (e t)")
                    link(dve.tensor_tensor_scan(fl(incl), fl(tot), fl(tot), 0.0, ALU.add, ALU.max))
                elif b == 4:
                    link(dve.tensor_tensor(base, incl, tot, ALU.subtract))
                    link(dve.tensor_tensor(count[:], incl[:, :, NT - 1], base[:, :, 0], ALU.subtract))
                    link(dve.tensor_scalar(count[:], count[:], float(P - 1), None, ALU.add))
                    link(dve.tensor_copy(count_i[:], count[:]))
                    link(dve.tensor_single_scalar(tiles_i[:], count_i[:], P.bit_length() - 1, ALU.arith_shift_right))
                elif b == 5:
                    link(dve.tensor_copy(tiles_f[:], tiles_i[:]))
                    link(dve.tensor_scalar(tiles_f[:], tiles_f[:], 1.0, None, ALU.max))
                    link(dve.tensor_tensor_scan(first_incl[:], tiles_f[:], tiles_f[:], 0.0, ALU.add, ALU.max))
                    link(dve.tensor_tensor(first_tile[:, 0:E], first_incl[:], tiles_f[:], ALU.subtract))
                    link(dve.tensor_copy(first_tile[:, E:E + 1], first_incl[:, E - 1:E]))
                    link(dve.scalar_tensor_tensor(off[:], first_tile[:, 0:E], float(P), base[:, :, 0],
                                                  ALU.mult, ALU.subtract))
                elif b == 6:
                    for e in range(E):
                        ins = dve.tensor_scalar(base[:, e, :], base[:, e, :], off[:, e:e + 1], None, ALU.add)
                    link(ins)
                elif b == 7:
                    for n, (t0, t1) in enumerate(pieces):
                        dve.wait_ge(piece_mm, len(pieces) + n + 1)
                        dve.tensor_tensor(cand[:, t0:t1], psY[n % 2][:, 0:(t1 - t0) * E].rearrange("p (t e) -> p t e", e=E),
                                          base[:, :, t0:t1].rearrange("p e t -> p t e"), ALU.add).then_inc(piece_read, 1)
                    dve.wait_ge(piece_read, 2 * len(pieces))

            def slots():
                link(dve.tensor_tensor(cand, cand, onehot[:], ALU.mult))
                link(dve.tensor_reduce(slot_f[:], cand, AX_X, ALU.add))
                link(dve.tensor_copy(slot[:], slot_f[:]))

            def one(c, j, it, more, more2):
                for b in range(NI):
                    if not more:
                        sort(b)
                    h_mul(c, b)
                    if b >= 1:
                        h_lo(c, b - 1)
                    if more and b % 2 == 0:
                        x_lo(*nxt(c, j, it), b // 2)
                    weights(c, b, lo)
                    if more2 and b >= NI - TILES:
                        stats_of(*nxt2(c, j, it), b - NI + TILES)
                h_lo(c, NI - 1)
                if more2:
                    moments(*nxt2(c, j, it))
                if more:
                    experts_out(*nxt(c, j, it))
                if more2:
                    normalise(*nxt2(c, j, it))
                if more:
                    route(*nxt(c, j, it))
                if not more:
                    slots()

            def start(c):
                for q in range(TILES):
                    stats_of(c, c, 0, q)
                moments(c, c, 0)

            start(0)
            normalise(0, 0, 0)
            lo("router")
            for q in range(TILES):
                x_lo(0, 0, 0, q)
            experts_out(0, 0, 0)
            lo((0, 0))
            lo((1, 0))
            start(1)
            route(0, 0, 0)
            normalise(1, 1, 0)
            chunks(dve, one)

        @block.tensor
        def _(pe):
            pe.wait_ge(const_done, 4)

            def transposes(c, j, it, q):
                pe.wait_ge(xn_done, c * TILES + q + 1)
                if not (isinstance(c, int) and c == 0):
                    pe.wait_ge(xlo_done, c * TILES + q)
                    if q == 0:
                        pe.wait_ge(logits_done, c)
                for kb in range(KD):
                    mm = pe.transpose(turned(c, q)[:, kb, :], xn[:, q, kb * P:(kb + 1) * P], ident[:])
                mm.then_inc(xpose_done, 1)

            def router(c, j, it):
                pe.wait_ge(xlo_done, (c + 1) * TILES)
                at_least(pe, by_expert_done, c)
                for kb in range(KD):
                    for a in range(2):
                        mm = pe.matmul(psL[:], rt[:, kb].rearrange("p h e -> p (h e)"), xT[j][:, a, kb, :],
                                       start=(kb == 0 and a == 0), stop=(kb == KD - 1 and a == 1))
                mm.then_inc(logits_mm, 1)

            def turn_logits(c, j, it):
                pe.wait_ge(by_expert_done, c + 1)
                settle(pe, settled)
                for q in range(TILES):
                    mm = pe.transpose(by_token[:, q, :], by_expert[:, q * P:(q + 1) * P], ident[0:2 * E, 0:2 * E])
                mm.then_inc(by_token_done, 1)

            def sort(b):
                cols = onehot[:].rearrange("p t e -> p (t e)")
                for w, b0, n0 in ((ones, 0, 0), (before, 5, len(pieces))):
                    here = range(2 * (b - b0), min(2 * (b - b0) + 2, len(pieces))) if b0 <= b < b0 + 2 else ()
                    for n in here:
                        t0, t1 = pieces[n]
                        if n0 + n == 0:
                            pe.wait_ge(sort_const, 5)
                            pe.wait_ge(onehot_done, NT)
                            pe.wait_ge(y_copied, (NCH - 1) * TILES)
                        at_least(pe, piece_read, n0 + n - 1)
                        pe.matmul(psY[n % 2][:, 0:(t1 - t0) * E], w[:], cols[:, t0 * E:t1 * E],
                                  start=True, stop=True).then_inc(piece_mm, 1)

            def one(c, j, it, more, more2):
                first = isinstance(c, int) and c == 0
                for b in range(NI):
                    cols = slice(b * P, (b + 1) * P)
                    for m, bank, done, freed in ((0, psG[b % 2], g_mm, sg_done), (1, psU[b % 2], u_mm, h_done)):
                        if first and b % 2 == 0:
                            pe.wait_ge(w_lo, order.index((m, b // 2)) + 1)
                        at_least(pe, freed, c * NI + b - 1)
                        for kb in range(KD):
                            mm = matmul_pairs(pe, bank[:], (gup[0][:, m, kb, cols], gup[1][:, m, kb, cols]),
                                              (xT[j][:, 0, kb, :], xT[j][:, 1, kb, :]), kb == 0, kb == KD - 1)
                        mm.then_inc(done, 1)
                    if more and b % 2 == 0:
                        transposes(*nxt(c, j, it), b // 2)
                    if not more:
                        sort(b)
                if more:
                    router(*nxt(c, j, it))
                if not more:
                    pe.wait_ge(piece_read, 2 * len(pieces))
                for q in range(TILES):
                    sl = slice(q * P, (q + 1) * P)
                    at_least(pe, y_copied, c * TILES + q - 1)
                    for kb in range(NI):
                        if q == 0:
                            pe.wait_ge(hlo_done, c * NI + kb + 1)
                            if first and kb % 2 == 0:
                                pe.wait_ge(w_lo, order.index(("down", kb // 2)) + 1)
                        mm = matmul_pairs(pe, psY[q % 2][:], (hT[:, 0, kb, sl], hT[:, 1, kb, sl]),
                                          (dnp[0][:, kb, :], dnp[1][:, kb, :]), kb == 0, kb == NI - 1)
                    mm.then_inc(y_mm, 1)
                    if more and q == 0:
                        turn_logits(*nxt(c, j, it))

            for q in range(TILES):
                transposes(0, 0, 0, q)
            pe.wait_ge(w_lo, 1)
            router(0, 0, 0)
            turn_logits(0, 0, 0)
            chunks(pe, one)


def recurrence_sweep(nc, z, xT, xT_dram, W1, b1s, W2, b2, i0, ss_dram, slot, token, tok_dram, first_tile,
                     tile_expert, tile_switch):
    KD, NB, D, B, NCH = z.KD, z.NB, z.D, z.B, z.NCH
    CPS = z.S // CHUNK
    assert CPS == 2 and B >= 2
    UPS = CPS * NB
    ss_t = ss_dram.rearrange("(t p) d -> t p d", p=P)
    GI, GF, GH = 2, 1, 0
    with ExitStack() as ctx:
        k = Kit(nc, ctx)
        w1 = [k.sb(f"w1_{h}", [P, KD, 3 * z.DIN], F32R) for h in ("hi", "lo")]
        w2 = [k.sb(f"w2_{h}", [P, NB, D], F32R) for h in ("hi", "lo")]
        w1v = W1.rearrange("(k p) n -> p k n", p=P)
        w2v = W2.rearrange("(k p) n -> p k n", p=P)

        def w1_part(w, kb):
            return w.rearrange("p k (g n) -> p k g n", g=3)[:, :, :, kb * P:(kb + 1) * P]

        nbf = k.sb("nbf", [P, NB])
        bh5 = k.sb("bh5", [P, NB])
        b2all = k.sb("b2all", [P, D])
        one_row = k.sb("one_row", [1, P])
        one = k.sb("one", [P, 1])
        start = k.sb("start", [P, NB])
        state = k.sb("state", [P, NB])
        L, E = z.PLACES + 1, z.E
        iota_t = k.sb("iota_t", [1, L])
        tile_f = k.sb("tile_f", [1, 2, L])
        diff = k.sb("diff", [1, 2, L - 1])
        i1, i2 = (k.sb(f"init{n}", [P, NB]) for n in range(2))
        isb = k.sb("isb", [P, CHUNK])
        m1 = k.sb("m1", [P, CHUNK])
        eu = k.sb("eu", [P, CHUNK])
        ev = k.sb("ev", [P, CHUNK])
        en = k.sb("en", [P, CHUNK])
        pa = k.sb("pa", [P, CHUNK])
        qb = k.sb("qb", [P, CHUNK])
        dn = k.sb("dn", [P, CHUNK])
        hm = k.sb("hm", [P, CHUNK])
        hp = k.sb("hp", [P, CHUNK])
        b2row = hp[0:1, 0:D]
        el = k.sb("el", [P, CHUNK])
        sd = k.sb("sd", [P, CHUNK])
        gg = k.sb("gg", [P, CHUNK])
        hs = k.sb("hs", [P, CHUNK])
        hT = k.sb("rhT", [P, 2, CHUNK], F32R)
        y = k.sb("ry", [P, TILES, D])
        assert KD * 3 * P <= 3 * D and TILES == 4
        raw1 = y[:, 0:3].rearrange("p q d -> p (q d)")[:, 0:KD * 3 * P].rearrange("p (k g n) -> p k g n", k=KD, g=3)
        raw2 = y[:, 3]
        gate = [k.ps(f"gate{n}", [P, CHUNK]) for n in range(4)]
        psY = [k.ps(f"rpsY{q}", [P, D]) for q in range(TILES)]

        small = k.sem("small")
        prep = k.sem("prep")
        names = ("i_mm f_mm h_mm out_mm isb_done m1_done du_done dv_done eu_done ev_done en_done q_done "
                 "p_done d_done ln_done r_done hm_done hp_done eh_done l_done sd_done sig_done g_done "
                 "a_done c_done b_done scan_done state_done hi_done lo_done y_mm y_done")
        s = {n: k.sem(f"rec_{n}") for n in names.split()}
        (i_mm, f_mm, h_mm, out_mm, isb_done, m1_done, du_done, dv_done, eu_done, ev_done, en_done, q_done,
         p_done, d_done, ln_done, r_done, hm_done, hp_done, eh_done, l_done, sd_done, sig_done, g_done,
         a_done, c_done, b_done, scan_done, state_done, hi_done, lo_done, y_mm, y_done) = \
            (s[n] for n in names.split())
        xT_loaded = [k.sem(f"rec_xT_loaded{j}") for j in range(2)]
        y_stored = [k.sem(f"rec_y_stored{q}") for q in range(TILES)]
        b2_mm = k.sem("b2_mm")
        places = k.sem("places")
        table_written = k.sem("table_written")
        settled = k.sem("settled2")
        w1_loaded, w2_loaded = k.sem("w1_loaded"), k.sem("w2_loaded")
        w1_hi, w1_lo, w2_hi, w2_lo = (k.sem(n) for n in ("w1_hi", "w1_lo", "w2_hi", "w2_lo"))

        def bias(g, kb):
            return b1s[:, g * NB + kb:g * NB + kb + 1]

        def sequences(eng, body):
            body(0, 0, True)
            with eng.Fori(1, B) as seq:
                body(seq * UPS, seq, False)

        block = ctx.enter_context(nc.Block())

        @block.sync
        def _(sp):
            for kk in range(KD):
                sp.dma_start(raw1[:, kk], w1_part(w1v, 0)[:, kk]).then_inc(w1_loaded, 16)
            sp.dma_start(b2row, b2.rearrange("(a n) -> a n", a=1)).then_inc(small, 16)
            sp.dma_start(raw2, w2v[:, 0, :]).then_inc(w2_loaded, 16)

            def load(c, j):
                sp.wait_ge(h_mm, (c - 1) * NB)
                sp.dma_start(xT[j][:].bitcast(F32), xT_dram[c - CPS]).then_inc(xT_loaded[j], 16)

            def store(c, place):
                for q in range(TILES):
                    sp.wait_ge(y_done, c * TILES + q + 1)
                    sp.dma_start(ss_t[place * TILES + q][:, D:2 * D], y[:, q]).then_inc(y_stored[q], 16)

            def load_weights(kb):
                sp.wait_ge(w2_lo, kb)
                for kk in range(KD):
                    sp.dma_start(raw1[:, kk], w1_part(w1v, kb)[:, kk]).then_inc(w1_loaded, 16)
                sp.dma_start(raw2, w2v[:, kb, :]).then_inc(w2_loaded, 16)

            for kb in range(1, NB):
                load_weights(kb)
            store(0, (B - 1) * CPS)
            load(2, 0)
            store(1, (B - 1) * CPS + 1)
            if B > 2:
                with sp.Fori(1, B - 1) as seq:
                    c0 = seq * CPS
                    load(c0 + 1, 1)
                    store(c0, c0 - CPS)
                    load(c0 + 2, 0)
                    store(c0 + 1, c0 + 1 - CPS)
            c0 = (B - 1) * CPS
            load(c0 + 1, 1)
            store(c0, c0 - CPS)
            store(c0 + 1, c0 + 1 - CPS)
            sp.wait_ge(table_written, 16 * z.NT)
            for q in range(TILES):
                sp.wait_ge(y_stored[q], 16 * NCH)

        @block.gpsimd
        def _(pool):
            pool.memset(one_row[:], 1.0).then_inc(prep, 1)
            pool.memset(one[:], 1.0).then_inc(prep, 1)
            pool.iota(iota_t[:], [[1, L]], base=0, channel_multiplier=0,
                      allow_small_or_imprecise_dtypes=True).then_inc(places, 1)

            def tail(U, kb):
                pool.wait_ge(scan_done, U + 1)
                settle(pool, settled)
                pool.tensor_copy(state[:, kb:kb + 1], hs[:, CHUNK - 1:CHUNK]).then_inc(state_done, 1)

            def body(u0, seq, first):
                for n in range(UPS):
                    U, kb = u0 + n, n % NB
                    if not (first and n == 0):
                        tail(U - 1, (n - 1) % NB)
                    if first:
                        for t in range(n * z.NT // UPS, (n + 1) * z.NT // UPS):
                            pool.indirect_dma_start(
                                out=tok_dram, out_offset=bass.IndirectOffsetOnAxis(ap=slot[:, t:t + 1], axis=0),
                                in_=token[:, t:t + 1], in_offset=None).then_inc(table_written, 16)
                    pool.wait_ge(p_done, U + 1)
                    pool.wait_ge(q_done, U + 1)
                    pool.wait_ge(a_done, U)
                    pool.wait_ge(c_done, U)
                    pool.tensor_tensor(dn[:], pa[:], qb[:], ALU.add).then_inc(d_done, 1)
                    pool.wait_ge(r_done, U + 1)
                    pool.tensor_tensor(qb[:], qb[:], dn[:], ALU.mult).then_inc(c_done, 1)

            sequences(pool, body)
            tail(B * UPS - 1, NB - 1)

        @block.scalar
        def _(act):
            act.preload_act_table_set("natural_log_exp_and_others")
            act.wait_ge(prep, 3)
            act.activation(i2[:], i1[:], ACT.Exp).then_inc(prep, 1)
            act.wait_ge(prep, 4)
            act.activation(i2[:], i2[:], ACT.Ln, bias=one[:, 0:1]).then_inc(prep, 1)
            act.wait_ge(prep, 6)
            act.activation(i2[:], i2[:], ACT.Exp).then_inc(prep, 1)
            act.wait_ge(prep, 11)

            def split(U):
                act.wait_ge(scan_done, U + 1)
                act.wait_ge(out_mm, U)
                act.activation(hT[:, 0, :], hs[:], ACT.Copy).then_inc(hi_done, 1)

            def hi(kb):
                act.wait_ge(w1_loaded, (kb + 1) * 16 * KD)
                round_hi(act, w1_part(w1[0][:], kb), raw1, w1_hi)
                act.wait_ge(w2_loaded, (kb + 1) * 16)
                round_hi(act, w2[0][:, kb, :], raw2, w2_hi)

            hi(0)

            def body(u0, seq, first):
                act.preload_act_table_set("natural_log_exp_and_others")
                for n in range(UPS):
                    U, kb = u0 + n, n % NB
                    act.wait_ge(i_mm, U + 1)
                    act.wait_ge(dv_done, U)
                    act.activation(isb[:], gate[(3 * n) % 4][:], ACT.Identity, bias=bias(GI, kb))\
                        .then_inc(isb_done, 1)
                    if not (first and n == 0):
                        split(U - 1)
                    act.wait_ge(m1_done, U + 1)
                    act.wait_ge(p_done, U)
                    act.wait_ge(q_done, U)
                    act.activation(en[:], m1[:], ACT.Exp).then_inc(en_done, 1)
                    act.wait_ge(du_done, U + 1)
                    act.activation(eu[:], eu[:], ACT.Exp, bias=nbf[:, kb:kb + 1]).then_inc(eu_done, 1)
                    act.wait_ge(dv_done, U + 1)
                    act.activation(ev[:], ev[:], ACT.Exp).then_inc(ev_done, 1)
                    act.wait_ge(h_mm, U + 1)
                    act.wait_ge(g_done, U)
                    act.activation(hp[:], gate[(3 * n + 2) % 4][:], ACT.Identity, bias=bh5[:, kb:kb + 1])\
                        .then_inc(hp_done, 1)
                    if first and n + 2 < NB:
                        hi(n + 2 if n else 1)
                    act.wait_ge(hm_done, U + 1)
                    act.wait_ge(sd_done, U)
                    act.activation(el[:], hm[:], ACT.Exp).then_inc(eh_done, 1)
                    act.wait_ge(eh_done, U + 1)
                    act.activation(el[:], el[:], ACT.Ln, bias=one[:, 0:1]).then_inc(l_done, 1)
                    act.wait_ge(d_done, U + 1)
                    act.activation(dn[:], dn[:], ACT.Ln).then_inc(ln_done, 1)
                    act.wait_ge(ln_done, U + 1)
                    act.activation(dn[:], dn[:], ACT.Exp, scale=-1.0).then_inc(r_done, 1)
                    act.wait_ge(sd_done, U + 1)
                    act.activation(sd[:], sd[:], ACT.Exp).then_inc(sig_done, 1)
                    if first and n == 0:
                        hi(2)

            sequences(act, body)
            split(B * UPS - 1)

        @block.vector
        def _(dve):
            dve.wait_ge(prep, 2)
            dve.tensor_scalar(i1[:], i0[:], 0.0, None, ALU.min).then_inc(prep, 1)
            dve.wait_ge(prep, 5)
            dve.tensor_tensor(i2[:], i1[:], i2[:], ALU.subtract).then_inc(prep, 1)
            dve.wait_ge(prep, 7)
            dve.scalar_tensor_tensor(start[:], i0[:], 0.5, i2[:], ALU.add, ALU.max).then_inc(prep, 1)
            dve.tensor_scalar(nbf[:], b1s[:, GF * NB:(GF + 1) * NB], -1.0, None, ALU.mult).then_inc(prep, 1)
            dve.tensor_scalar(bh5[:], b1s[:, GH * NB:(GH + 1) * NB], 0.5, None, ALU.add).then_inc(prep, 1)
            dve.wait_ge(b2_mm, 1)
            dve.tensor_copy(b2all[:], psY[0][:]).then_inc(prep, 1)
            dve.wait_ge(prep, 11)

            def scan(U, n):
                kb = n % NB
                dve.wait_ge(c_done, U + 1)
                dve.wait_ge(g_done, U + 1)
                dve.tensor_tensor(qb[:], qb[:], gg[:], ALU.mult).then_inc(b_done, 1)
                dve.wait_ge(b_done, U + 1)
                dve.wait_ge(a_done, U + 1)
                dve.wait_ge(state_done, U)
                dve.wait_ge(hi_done, U)
                dve.wait_ge(lo_done, U)
                first = start if n < NB else state
                dve.tensor_tensor_scan(hs[:], pa[:], qb[:], first[:, kb:kb + 1], ALU.mult, ALU.add)\
                    .then_inc(scan_done, 1)

            def split(U):
                dve.wait_ge(hi_done, U + 1)
                dve.tensor_tensor(hT[:, 1, :], hs[:], hT[:, 0, :], ALU.subtract).then_inc(lo_done, 1)

            def output(c):
                for q in range(TILES):
                    if q < TILES - 1:
                        dve.wait_ge(y_mm, c * (TILES - 1) + q + 1)
                    else:
                        dve.wait_ge(out_mm, (c + 1) * NB)
                    dve.wait_ge(y_stored[q], c * 16)
                    dve.tensor_tensor(y[:, q], psY[q][:], b2all[:], ALU.add).then_inc(y_done, 1)

            def lo(kb):
                dve.wait_ge(w1_hi, kb + 1)
                leave_lo(dve, w1_part(w1[1][:], kb), raw1, w1_part(w1[0][:], kb), w1_lo)
                dve.wait_ge(w2_hi, kb + 1)
                leave_lo(dve, w2[1][:, kb, :], raw2, w2[0][:, kb, :], w2_lo)

            lo(0)

            dve.memset(tile_f[:, 0, :], -1.0).then_inc(places, 1)
            last = tile_f[:, (E + 1) % 2, :]

            def count_starts(e):
                dve.wait_ge(places, e + 2)
                dve.scalar_tensor_tensor(tile_f[:, (e + 1) % 2, :], iota_t[:], first_tile[0:1, e:e + 1],
                                         tile_f[:, e % 2, :], ALU.is_ge, ALU.add).then_inc(places, 1)

            def finish_places():
                dve.wait_ge(places, E + 3)
                dve.tensor_copy(tile_expert[:, 0:L], last).then_inc(places, 1)
                dve.tensor_copy(tile_expert[:, L:L + 1], first_tile[0:1, E:E + 1]).then_inc(places, 1)
                dve.tensor_tensor(diff[:, 0], last[:, 1:L], last[:, 0:L - 1], ALU.subtract).then_inc(places, 1)
                dve.wait_ge(places, E + 6)
                dve.scalar_tensor_tensor(diff[:, 1], last[:, 1:L], float(E), diff[:, 0], ALU.is_lt, ALU.mult)\
                    .then_inc(places, 1)
                dve.wait_ge(places, E + 7)
                dve.tensor_copy(tile_switch[:], diff[:, 1]).then_inc(places, 1)
                dve.wait_ge(places, E + 8)

            def body(u0, seq, first):
                for n in range(UPS):
                    U, kb = u0 + n, n % NB
                    lag = not (first and n == 0)
                    if lag:
                        scan(U - 1, (n - 1) % UPS)
                    dve.wait_ge(f_mm, U + 1)
                    dve.wait_ge(isb_done, U + 1)
                    dve.wait_ge(en_done, U)
                    dve.wait_ge(du_done, U)
                    dve.wait_ge(dv_done, U)
                    psF = gate[(3 * n + 1) % 4]
                    dve.scalar_tensor_tensor(m1[:], psF[:], bias(GF, kb), isb[:], ALU.add, ALU.min)\
                        .then_inc(m1_done, 1)
                    if lag:
                        split(U - 1)
                    dve.wait_ge(m1_done, U + 1)
                    dve.wait_ge(q_done, U)
                    dve.scalar_tensor_tensor(eu[:], m1[:], 0.0, psF[:], ALU.min, ALU.subtract)\
                        .then_inc(du_done, 1)
                    dve.wait_ge(p_done, U)
                    dve.scalar_tensor_tensor(ev[:], m1[:], 0.0, isb[:], ALU.min, ALU.subtract)\
                        .then_inc(dv_done, 1)
                    dve.wait_ge(en_done, U + 1)
                    dve.wait_ge(eu_done, U + 1)
                    dve.wait_ge(scan_done, U)
                    dve.scalar_tensor_tensor(qb[:], en[:], 1.0, eu[:], ALU.min, ALU.add).then_inc(q_done, 1)
                    dve.wait_ge(ev_done, U + 1)
                    dve.scalar_tensor_tensor(pa[:], en[:], 1.0, ev[:], ALU.min, ALU.add).then_inc(p_done, 1)
                    dve.wait_ge(hp_done, U + 1)
                    dve.wait_ge(eh_done, U)
                    dve.wait_ge(sd_done, U)
                    dve.tensor_scalar(hm[:], gate[(3 * n + 2) % 4][:], bias(GH, kb), 0.0, ALU.add, ALU.min)\
                        .then_inc(hm_done, 1)
                    if first and n + 2 < NB:
                        lo(n + 2 if n else 1)
                    if kb == 0 and not (first and n == 0):
                        output(seq * CPS + n // NB - 1)
                    dve.wait_ge(hm_done, U + 1)
                    dve.wait_ge(l_done, U + 1)
                    dve.wait_ge(g_done, U)
                    dve.tensor_tensor(sd[:], hm[:], el[:], ALU.subtract).then_inc(sd_done, 1)
                    dve.wait_ge(r_done, U + 1)
                    dve.wait_ge(d_done, U + 1)
                    dve.tensor_tensor(pa[:], pa[:], dn[:], ALU.mult).then_inc(a_done, 1)
                    dve.wait_ge(sig_done, U + 1)
                    dve.wait_ge(hp_done, U + 1)
                    dve.wait_ge(b_done, U)
                    dve.tensor_tensor(gg[:], hp[:], sd[:], ALU.max).then_inc(g_done, 1)
                    if first and n == 0:
                        lo(2)
                    if first:
                        for e in range(n * (E + 1) // UPS, (n + 1) * (E + 1) // UPS):
                            count_starts(e)

            sequences(dve, body)
            scan(B * UPS - 1, UPS - 1)
            split(B * UPS - 1)
            output(NCH - 1)
            finish_places()

        @block.tensor
        def _(pe):
            pe.wait_ge(small, 16)
            pe.wait_ge(prep, 2)
            pe.matmul(psY[0][:], one_row[:], b2row, start=True, stop=True).then_inc(b2_mm, 1)
            pe.wait_ge(prep, 11)

            def outputs(U, n, c):
                kb = n % NB
                pe.wait_ge(hi_done, U + 1)
                if isinstance(U, int) and U < NB:
                    pe.wait_ge(w2_lo, U + 1)
                if kb == 0:
                    pe.wait_ge(y_done, c * TILES)
                for q in range(TILES):
                    for w in w2:
                        pe.matmul(psY[q][:], hT[:, 0, q * P:(q + 1) * P], w[:, kb, :],
                                  start=kb == 0 and w is w2[0], stop=False)
                pe.wait_ge(lo_done, U + 1)
                for q in range(TILES):
                    mm = pe.matmul(psY[q][:], hT[:, 1, q * P:(q + 1) * P], w2[0][:, kb, :],
                                   start=False, stop=kb == NB - 1)
                    if kb == NB - 1 and q < TILES - 1:
                        mm.then_inc(y_mm, 1)
                mm.then_inc(out_mm, 1)

            def body(u0, seq, first):
                for n in range(UPS):
                    U, kb, j = u0 + n, n % NB, n // NB
                    if kb == 0:
                        at_least(pe, xT_loaded[j], seq * 16)
                    if first and n < NB:
                        pe.wait_ge(w1_lo, n + 1)
                    for g, third, done, freed in ((0, GI, i_mm, None), (1, GF, f_mm, isb_done), (2, GH, h_mm, du_done)):
                        bank = gate[(3 * n + g) % 4]
                        if g > 0:
                            pe.wait_ge(freed, U)
                        elif not (first and n < 2):
                            pe.wait_ge(hm_done, U - 1)
                            pe.wait_ge(hp_done, U - 1)
                        cols = slice(third * z.DIN + kb * P, third * z.DIN + (kb + 1) * P)
                        for kk in range(KD):
                            mm = matmul_pairs(pe, bank[:], (w1[0][:, kk, cols], w1[1][:, kk, cols]),
                                              (xT[j][:, 0, kk, :], xT[j][:, 1, kk, :]), kk == 0, kk == KD - 1)
                        mm.then_inc(done, 1)
                    if not (first and n == 0):
                        outputs(U - 1, (n - 1) % UPS, seq * CPS + (n - 1) // NB)

            sequences(pe, body)
            outputs(B * UPS - 1, UPS - 1, NCH - 1)


def routed_sweep(nc, z, x, rgw, ruw, rdw, xs_dram, ss_dram, tok_dram, tile_expert, tile_switch,
                 ident, out):
    KD, NI, D, E, NS, T = z.KD, z.NI, z.D, z.E, z.NS, z.T
    HALF = z.I // 2
    KH = NI // 2
    PARTS = 6
    G0, U0, G1, U1, D0, D1 = range(PARTS)
    BY_POOL = (U0, D0)
    x_rows = x.rearrange("b s d -> (b s) d")
    out_rows = out.rearrange("b s d -> (b s) d")
    with ExitStack() as ctx:
        k = Kit(nc, ctx)
        raw = [k.sb(f"raw{q}", [P, 4, 512]) for q in range(PARTS)]
        whi = [k.sb(f"whi{q}", [P, 4, 512], F32R) for q in range(PARTS)]
        wlo = [k.sb(f"wlo{q}", [P, 4, 512], F32R) for q in range(PARTS)]
        xg = k.sb("xg", [P, D])
        xT = k.sb("txT", [P, 2, KD, P], F32R)
        sg = [k.sb(f"tsg{n}", [P, HALF]) for n in range(2)]
        h = [k.sb(f"th{n}", [P, HALF]) for n in range(2)]
        hT = [k.sb(f"thT{n}", [P, 2, KH, P], F32R) for n in range(2)]
        ss = k.sb("shared_and_s", [P, 2 * D])
        xr = k.sb("xr", [P, D])
        zb = k.sb("zb", [P, D])
        yo = k.sb("yo", [P, D])
        back_i = k.sb("back_i", [NS, P], I32)
        back = k.sb("back", [NS, P])
        clipped = k.sb("clipped", [P, NS])
        gather_at = k.sb("gather_at", [P, z.PLACES + 1], I32)
        scatter_at = k.sb("scatter_at", [P, z.PLACES], I32)
        at_next = k.sb("at_next", [P, 1], I32)
        at_this = k.sb("at_this", [P, 1], I32)
        at_out = k.sb("at_out", [P, 1], I32)
        psG = [k.ps(f"tG{n}", [P, HALF]) for n in range(2)]
        psU = [k.ps(f"tU{n}", [P, HALF]) for n in range(2)]
        psX = k.ps("tX", [P, KD, P])
        psH = [k.ps(f"tH{n}", [P, KH, P]) for n in range(2)]
        psY = k.ps("tY", [P, D])

        raw_loaded = [k.sem(f"raw_loaded{q}") for q in range(PARTS)]
        whi_done = [k.sem(f"whi_done{q}") for q in range(PARTS)]
        wlo_done = [k.sem(f"wlo_done{q}") for q in range(PARTS)]
        used = [k.sem(f"used{q}") for q in range(PARTS)]
        settled = k.sem("settled")
        returned = k.sem("returned")
        back_done = k.sem("back_done")
        turned_table = k.sem("turned_table")
        table = k.sem("table")
        at_done = k.sem("at_done")
        at_out_done = k.sem("at_out_done")
        xg_loaded = k.sem("xg_loaded")
        ss_loaded = k.sem("ss_loaded")
        xr_loaded = k.sem("xr_loaded")
        out_stored = k.sem("out_stored")
        turned_x = k.sem("turned_x")
        xhi = k.sem("txhi")
        xlo = k.sem("txlo")
        sg_done = [k.sem(f"tsg_done{n}") for n in range(2)]
        h_done = [k.sem(f"th_done{n}") for n in range(2)]
        turned_h = [k.sem(f"turned_h{n}") for n in range(2)]
        hhi = [k.sem(f"thhi{n}") for n in range(2)]
        hlo = [k.sem(f"thlo{n}") for n in range(2)]
        z_done = k.sem("z_done")
        zs_done = k.sem("zs_done")
        zm_done = k.sem("zm_done")
        yo_done = k.sem("yo_done")
        block = ctx.enter_context(nc.Block())

        def tiles(eng, body, switches=True):
            def one(t, e):
                if not switches:
                    return body(t, e, False)
                s = eng.value_load(tile_switch[0:1, bass.ds(t, 1)], min_val=0, max_val=1)
                with eng.If(s > 0):
                    body(t, e, True)
                with eng.Else():
                    body(t, e, False)

            one(0, 0)
            with eng.Fori(0, z.GROUPS) as g:
                e0 = eng.value_load(tile_expert[0:1, bass.ds(g * GROUP + 1, 1)], min_val=0, max_val=E)
                with eng.If(e0 < E):
                    with eng.Fori(1, GROUP + 1) as r:
                        t = g * GROUP + r
                        e = eng.value_load(tile_expert[0:1, bass.ds(t, 1)], min_val=0, max_val=E)
                        with eng.If(e < E):
                            one(t, e)

        def part(q, e):
            if q < D0:
                w = (rgw, ruw)[q % 2][e].rearrange("(k p) i -> p k i", p=P)
                return w[:, :, (q // 2) * HALF:(q // 2 + 1) * HALF]
            return rdw[e].rearrange("(k p) d -> p k d", p=P)[:, (q - D0) * KH:(q - D0 + 1) * KH, :]

        @block.sync
        def _(sp):
            sp.dma_start(back_i[:], tok_dram.rearrange("(s p) a -> s (p a)", p=P)).then_inc(returned, 16)
            for q in range(PARTS):
                if q == 1:
                    sp.wait_ge(xg_loaded, 16)
                sp.dma_start(raw[q][:], part(q, 0)).then_inc(raw_loaded[q], 16)
            with sp.Fori(1, E) as e:
                for q in range(PARTS):
                    sp.wait_ge(wlo_done[q], e)
                    sp.dma_start(raw[q][:], part(q, e)).then_inc(raw_loaded[q], 16)

        def split_hi(act, q, e, t):
            act.wait_ge(raw_loaded[q], (e + 1) * 16)
            if t is not None:
                act.wait_ge(used[q], t + 1)
            act.activation(whi[q][:], raw[q][:], ACT.Copy).then_inc(whi_done[q], 1)

        def split_lo(eng, q, e):
            eng.wait_ge(whi_done[q], e + 1)
            eng.tensor_tensor(wlo[q][:], raw[q][:], whi[q][:], ALU.subtract).then_inc(wlo_done[q], 1)

        @block.gpsimd
        def _(pool):
            def fetch(dst, src, at, done):
                pool.indirect_dma_start(out=dst, out_offset=None, in_=src,
                                        in_offset=bass.IndirectOffsetOnAxis(ap=at, axis=0)).then_inc(done, 16)

            def scatter(t):
                pool.wait_ge(yo_done, t + 1)
                settle(pool, settled)
                pool.tensor_copy(at_out[:], scatter_at[:, bass.ds(t, 1)]).then_inc(at_out_done, 1)
                pool.wait_ge(at_out_done, t + 1)
                settle(pool, settled)
                pool.indirect_dma_start(out=out_rows, out_offset=bass.IndirectOffsetOnAxis(ap=at_out[:], axis=0),
                                        in_=yo[:], in_offset=None, bounds_check=T - 1,
                                        oob_is_err=False).then_inc(out_stored, 16)

            pool.wait_ge(table, 4)
            pool.tensor_copy(at_next[:], gather_at[:, 0:1]).then_inc(at_done, 1)
            pool.wait_ge(at_done, 1)
            fetch(xg[:], xs_dram, at_next[:], xg_loaded)
            split_lo(pool, U0, 0)

            def body(t, e, switch):
                pool.wait_ge(xg_loaded, (t + 1) * 16)
                settle(pool, settled)
                pool.tensor_copy(at_next[:], gather_at[:, bass.ds(t + 1, 1)]).then_inc(at_done, 1)
                pool.wait_ge(at_done, t * 2 + 2)
                pool.wait_ge(turned_x, t + 1)
                settle(pool, settled)
                fetch(xg[:], xs_dram, at_next[:], xg_loaded)
                if not isinstance(t, int):
                    scatter(t - 1)
                at_least(pool, ss_loaded, t * 16)
                at_least(pool, xr_loaded, t * 16)
                settle(pool, settled)
                pool.tensor_copy(at_this[:], gather_at[:, bass.ds(t, 1)]).then_inc(at_done, 1)
                pool.wait_ge(at_done, t * 2 + 3)
                settle(pool, settled)
                fetch(ss[:], ss_dram, at_this[:], ss_loaded)
                fetch(xr[:], x_rows, at_this[:], xr_loaded)
                if isinstance(t, int):
                    split_lo(pool, D0, 0)
                if switch:
                    split_lo(pool, U0, e + 1)
                    split_lo(pool, D0, e + 1)

            tiles(pool, body)
            total = pool.value_load(tile_expert[0:1, z.PLACES + 1:z.PLACES + 2], min_val=1, max_val=NS)
            scatter(total - 1)
            pool.wait_ge(out_stored, total * 16)
            settle(pool, settled)
            pool.memset(at_out[:], 0).then_inc(at_done, 1)

        @block.scalar
        def _(act):
            def x_hi(t):
                act.wait_ge(turned_x, t + 1)
                at_least(act, used[U1], t)
                act.activation(xT[:, 0], psX[:], ACT.Copy).then_inc(xhi, 1)

            split_hi(act, G0, 0, None)
            x_hi(0)
            for q in (U0, G1):
                split_hi(act, q, 0, None)

            def first_split(t, *qs):
                if isinstance(t, int):
                    for q in qs:
                        split_hi(act, q, 0, None)

            def body(t, e, switch):
                def silu(n):
                    act.wait_ge(used[(G0, G1)[n]], t + 1)
                    at_least(act, h_done[n], t)
                    act.activation(sg[n][:], psG[n][:], ACT.Silu).then_inc(sg_done[n], 1)

                def h_hi(n):
                    act.wait_ge(turned_h[n], t + 1)
                    at_least(act, used[(D0, D1)[n]], t)
                    act.activation(hT[n][:, 0], psH[n][:], ACT.Copy).then_inc(hhi[n], 1)

                def hi(q):
                    if switch:
                        split_hi(act, q, e + 1, t)

                silu(0)
                first_split(t, U1)
                hi(G0)
                hi(U0)
                silu(1)
                h_hi(0)
                first_split(t, D0, D1)
                hi(G1)
                hi(U1)
                h_hi(1)
                x_hi(t + 1)
                hi(D0)
                act.wait_ge(z_done, t + 1)
                act.activation(zb[:], zb[:], ACT.Silu).then_inc(zs_done, 1)
                hi(D1)

            tiles(act, body)

        @block.vector
        def _(dve):
            def lo(q, e):
                if q not in BY_POOL:
                    split_lo(dve, q, e)

            def x_lo(t):
                dve.wait_ge(xhi, t + 1)
                dve.tensor_tensor(xT[:, 1], psX[:], xT[:, 0], ALU.subtract).then_inc(xlo, 1)

            dve.wait_ge(returned, 16)
            dve.tensor_copy(back[:], back_i[:]).then_inc(back_done, 1)
            dve.wait_ge(turned_table, 1)
            dve.tensor_copy(scatter_at[:, 0:NS], psY[:, 0:NS]).then_inc(table, 1)
            dve.tensor_scalar(clipped[:], psY[:, 0:NS], float(T - 1), None, ALU.min).then_inc(table, 1)
            dve.memset(gather_at[:, NS:NS + 1], 0).then_inc(table, 1)
            dve.wait_ge(table, 3)
            dve.tensor_copy(gather_at[:, 0:NS], clipped[:]).then_inc(table, 1)
            lo(G0, 0)
            x_lo(0)
            lo(G1, 0)

            def body(t, e, switch):
                def h_mul(n):
                    dve.wait_ge(sg_done[n], t + 1)
                    dve.wait_ge(used[(U0, U1)[n]], t + 1)
                    at_least(dve, turned_h[n], t)
                    dve.tensor_tensor(h[n][:], sg[n][:], psU[n][:], ALU.mult).then_inc(h_done[n], 1)

                def h_lo(n):
                    dve.wait_ge(hhi[n], t + 1)
                    dve.tensor_tensor(hT[n][:, 1], psH[n][:], hT[n][:, 0], ALU.subtract).then_inc(hlo[n], 1)

                def nxt(q):
                    if switch:
                        lo(q, e + 1)

                h_mul(0)
                if isinstance(t, int):
                    lo(U1, 0)
                nxt(G0)
                h_lo(0)
                if isinstance(t, int):
                    lo(D1, 0)
                h_mul(1)
                nxt(G1)
                h_lo(1)
                x_lo(t + 1)
                nxt(U1)
                dve.wait_ge(used[D1], t + 1)
                dve.wait_ge(ss_loaded, (t + 1) * 16)
                at_least(dve, zm_done, t)
                dve.tensor_tensor(zb[:], psY[:], ss[:, 0:D], ALU.add).then_inc(z_done, 1)
                dve.wait_ge(zs_done, t + 1)
                at_least(dve, out_stored, t * 16)
                dve.tensor_tensor(yo[:], zb[:], ss[:, D:2 * D], ALU.mult).then_inc(zm_done, 1)
                dve.wait_ge(zm_done, t + 1)
                dve.wait_ge(xr_loaded, (t + 1) * 16)
                dve.tensor_tensor(yo[:], yo[:], xr[:], ALU.add).then_inc(yo_done, 1)
                nxt(D1)

            tiles(dve, body)

        @block.tensor
        def _(pe):
            def turn_x(t):
                pe.wait_ge(xg_loaded, (t + 1) * 16)
                at_least(pe, xlo, t)
                for kb in range(KD):
                    mm = pe.transpose(psX[:, kb, :], xg[:, kb * P:(kb + 1) * P], ident[:])
                mm.then_inc(turned_x, 1)

            pe.wait_ge(back_done, 1)
            pe.transpose(psY[:, 0:NS], back[:], ident[0:NS, 0:NS]).then_inc(turned_table, 1)
            pe.wait_ge(table, 2)
            turn_x(0)

            def body(t, e, switch):
                def up(q, bank, freed):
                    pe.wait_ge(wlo_done[q], e + 1)
                    at_least(pe, freed, t)
                    for kb in range(KD):
                        mm = matmul_pairs(pe, bank[:], (xT[:, 0, kb, :], xT[:, 1, kb, :]),
                                          (whi[q][:, kb, :], wlo[q][:, kb, :]), kb == 0, kb == KD - 1)
                    mm.then_inc(used[q], 1)

                def turn_h(n):
                    pe.wait_ge(h_done[n], t + 1)
                    at_least(pe, hlo[n], t)
                    for kb in range(KH):
                        mm = pe.transpose(psH[n][:, kb, :], h[n][:, kb * P:(kb + 1) * P], ident[:])
                    mm.then_inc(turned_h[n], 1)

                def down(n, lows, blocks):
                    q = (D0, D1)[n]
                    for kb in blocks:
                        for w in (whi[q],) if lows else (whi[q], wlo[q]):
                            mm = pe.matmul(psY[:], hT[n][:, int(lows), kb, :], w[:, kb, :],
                                           start=n == 0 and kb == 0 and not lows and w is whi[q],
                                           stop=n == 1 and kb == KH - 1 and lows)
                    return mm

                pe.wait_ge(xlo, t + 1)
                up(G0, psG[0], sg_done[0])
                up(U0, psU[0], h_done[0])
                up(G1, psG[1], sg_done[1])
                turn_h(0)
                up(U1, psU[1], h_done[1])
                turn_x(t + 1)
                pe.wait_ge(wlo_done[D0], e + 1)
                pe.wait_ge(hlo[0], t + 1)
                at_least(pe, z_done, t)
                down(0, False, range(KH))
                turn_h(1)
                down(0, True, range(KH)).then_inc(used[D0], 1)
                pe.wait_ge(wlo_done[D1], e + 1)
                pe.wait_ge(hhi[1], t + 1)
                down(1, False, range(KH))
                pe.wait_ge(hlo[1], t + 1)
                down(1, True, range(KH)).then_inc(used[D1], 1)

            tiles(pe, body, switches=False)


def moe_recurrent_kernel(nc, x, W1, b1, W2, b2, init_h, gate_w, sgw, suw, sdw, rgw, ruw, rdw, out):
    z = Shapes(x, W1, gate_w, sgw)
    xT_dram = nc.dram_tensor("xT_dram", [z.NCH, P, 2, z.KD, CHUNK], F32).ap()
    xs_dram = nc.dram_tensor("xs_dram", [z.T, z.D], F32).ap()
    ss_dram = nc.dram_tensor("ss_dram", [z.T, 2 * z.D], F32).ap()
    tok_dram = nc.dram_tensor("tok_dram", [z.NS * P, 1], I32).ap()
    with ExitStack() as ctx:
        k = Kit(nc, ctx)
        ident = k.sb("ident", [P, P])
        b1s = k.sb("b1s", [P, 3 * z.NB])
        i0 = k.sb("init_h_by_channel", [P, z.NB])
        slot = k.sb("slot", [P, z.NT], I32)
        token = k.sb("token", [P, z.NT], I32)
        first_tile = k.sb("first_tile", [P, z.E + 1])
        tile_expert = k.sb("tile_expert", [1, z.PLACES + 2], I32)
        tile_switch = k.sb("tile_switch", [1, z.PLACES], I32)
        transposed = k.ctx.enter_context(ExitStack())
        xT = [transposed.enter_context(nc.sbuf_tensor(f"xT{j}", [P, 2, z.KD, CHUNK], F32R)) for j in range(2)]
        with nc.sbuf_tensor("onehot", [P, z.NT, z.E], BF16) as onehot:
            shared_sweep(nc, z, x, gate_w, sgw, suw, sdw, xT, xT_dram, xs_dram, ss_dram, onehot, ident,
                         tok_dram, slot, token, first_tile, b1, b1s, init_h, i0)
        recurrence_sweep(nc, z, xT, xT_dram, W1, b1s, W2, b2, i0, ss_dram, slot, token, tok_dram, first_tile,
                         tile_expert, tile_switch)
        transposed.close()
        routed_sweep(nc, z, x, rgw, ruw, rdw, xs_dram, ss_dram, tok_dram, tile_expert, tile_switch,
                     ident, out)


_INS = ["L0_attn_x", "L0_attn_W1", "L0_attn_b1", "L0_attn_W2", "L0_attn_b2", "L0_attn_init_h",
        "L0_ffn_gate_w", "L0_ffn_shared_gate_w", "L0_ffn_shared_up_w", "L0_ffn_shared_down_w",
        "L0_ffn_routed_gate_w", "L0_ffn_routed_up_w", "L0_ffn_routed_down_w"]


def kernel(**inputs):
    import numpy as np
    import concourse.bacc as bacc
    from concourse.bass_utils import run_bass_kernel_spmd

    nc = bacc.Bacc("TRN2", target_bir_lowering=False, num_devices=1)
    arrays, args = {}, []
    for name in _INS:
        a = np.ascontiguousarray(inputs[name])
        arrays[f"in_{name}"] = a
        args.append(nc.dram_tensor(f"in_{name}", a.shape, mybir.dt.from_np(a.dtype), kind="ExternalInput").ap())
    args.append(nc.dram_tensor("out_0", inputs["L0_attn_x"].shape, F32, kind="ExternalOutput").ap())
    moe_recurrent_kernel(nc, *args)
    r = run_bass_kernel_spmd(nc, [arrays], core_ids=[0])
    return r.results[0]["out_0"]
```
